# Optimizing a Trainium2 kernel written in Bass

```python
import numpy as np
import jax
import jax.numpy as jnp

def _softmax(x, axis=-1):
    return jax.nn.softmax(x, axis=axis)

def _gelu(x):
    return jax.nn.gelu(x, approximate=True)

def _silu(x):
    return jax.nn.silu(x)

def _sigmoid(x):
    return jax.nn.sigmoid(x)

def _layernorm(x, axis=-1, eps=1e-05):
    m = jnp.mean(x, axis=axis, keepdims=True)
    v = jnp.var(x, axis=axis, keepdims=True)
    return (x - m) / jnp.sqrt(v + eps)

def _scatter_add(tgt, idx, src, axis=0):
    return tgt.at[idx].add(src)

def _segment_sum(src, seg, n):
    return jax.ops.segment_sum(src, seg, n)
kernel_name = 'mk_decoder_postln_d1_seqx_r8_050713'

def setup_inputs(seed: int=0):
    np.random.seed(seed)
    _w = jnp.asarray

    def _rec_inputs():
        import jax
        import jax.numpy as jnp
        _rk = jax.random.key(seed)
        x = -0.0002928 + 1 * jax.random.normal(jax.random.fold_in(_rk, 1), (4, 512, 128), jnp.float32)
        _lenS = 512 - jax.random.randint(jax.random.fold_in(_rk, 7), (4,), 0, max(1, 512 // 4) + 1, jnp.int32)
        _lenS2 = 32 - jax.random.randint(jax.random.fold_in(_rk, 8), (4,), 0, max(1, 32 // 4) + 1, jnp.int32)
        _ctx_1024P = jax.random.normal(jax.random.fold_in(_rk, 11), (4, 16, 128), jnp.float32)
        _ctx_1024c = jax.random.dirichlet(jax.random.fold_in(_rk, 511), 0.3 * jnp.ones((16,), jnp.float32), (4, 32))
        _ctx_1024t = jnp.einsum('bsk,bkd->bsd', _ctx_1024c, _ctx_1024P)
        _ctx_1024t = _ctx_1024t * jax.lax.rsqrt(jnp.mean(jnp.square(_ctx_1024t)) + 1e-12) * 0.953939
        ctx_1024 = -1.39393e-06 + 0.999914 * (_ctx_1024t + 0.3 * jax.random.normal(jax.random.fold_in(_rk, 611), (4, 32, 128), jnp.float32))
        return (x, ctx_1024)
    x, ctx_1024 = _rec_inputs()

    def _L0_attn_setup():
        import jax, jax.numpy as jnp
        import numpy as np
        B, T, D_MODEL = (4, 512, 128)
        H = 16
        DH = D_MODEL // H
        EPS = 1e-06
        CHUNK = 128

        def _feature(x):
            return jnp.where(x > 0, x + 1.0, jnp.exp(x))

        def _causal_dot_product(Q, K, V):
            b, h, t, d = Q.shape
            nc = t // CHUNK
            mask = jnp.tril(jnp.ones((CHUNK, CHUNK), dtype=Q.dtype))
            qs = jnp.moveaxis(Q.reshape(b, h, nc, CHUNK, d), 2, 0)
            ks = jnp.moveaxis(K.reshape(b, h, nc, CHUNK, d), 2, 0)
            vs = jnp.moveaxis(V.reshape(b, h, nc, CHUNK, d), 2, 0)

            def step(S, qkv):
                q, k, v = qkv
                attn = jnp.einsum('bhid,bhjd->bhij', q, k) * mask
                out = jnp.einsum('bhij,bhjd->bhid', attn, v) + jnp.einsum('bhid,bhde->bhie', q, S)
                S = S + jnp.einsum('bhcd,bhce->bhde', k, v)
                return (S, out)
            S0 = jnp.zeros((b, h, d, d), dtype=Q.dtype)
            _, outs = jax.lax.scan(step, S0, (qs, ks, vs))
            return jnp.moveaxis(outs, 0, 2).reshape(b, h, t, d)
        key = jax.random.key(seed)
        ks = jax.random.split(key, 6)
        s = 0.02
        x = jax.random.normal(ks[0], (B, T, D_MODEL), dtype=jnp.float32)
        Wq = jax.random.normal(ks[1], (D_MODEL, D_MODEL), dtype=jnp.float32) * s
        Wk = jax.random.normal(ks[2], (D_MODEL, D_MODEL), dtype=jnp.float32) * s
        Wv = jax.random.normal(ks[3], (D_MODEL, D_MODEL), dtype=jnp.float32) * s
        Wo = jax.random.normal(ks[4], (D_MODEL, D_MODEL), dtype=jnp.float32) * s
        bo = jax.random.normal(ks[5], (D_MODEL,), dtype=jnp.float32) * s
        return {'x': x, 'Wq': Wq, 'Wk': Wk, 'Wv': Wv, 'Wo': Wo, 'bo': bo}
    _L0_attn_all = _L0_attn_setup()
    _L0_attn_in = {k: v for k, v in _L0_attn_all.items() if k in ('Wq', 'Wk', 'Wv', 'Wo', 'bo')}
    del _L0_attn_all

    def _L0_xattn_setup():
        import jax, jax.numpy as jnp
        import numpy as np
        H = 16
        D = 64
        key = jax.random.key(seed)
        ks = jax.random.split(key, 11)
        b, n, dm = (2, 256, 128)
        s = 1.0 / np.sqrt(dm)
        return {'q': jax.random.normal(ks[0], (b, n, dm), jnp.float32), 'k': jax.random.normal(ks[1], (b, n, dm), jnp.float32), 'v': jax.random.normal(ks[2], (b, n, dm), jnp.float32), 'Wq': jax.random.normal(ks[3], (dm, H * D), jnp.float32) * s, 'bq': jax.random.normal(ks[4], (H * D,), jnp.float32) * 0.01, 'Wk': jax.random.normal(ks[5], (dm, H * D), jnp.float32) * s, 'bk': jax.random.normal(ks[6], (H * D,), jnp.float32) * 0.01, 'Wv': jax.random.normal(ks[7], (dm, H * D), jnp.float32) * s, 'bv': jax.random.normal(ks[8], (H * D,), jnp.float32) * 0.01, 'Wo': jax.random.normal(ks[9], (H * D, dm), jnp.float32) * s, 'bo': jax.random.normal(ks[10], (dm,), jnp.float32) * 0.01}
    _L0_xattn_all = _L0_xattn_setup()
    _L0_xattn_in = {k: v for k, v in _L0_xattn_all.items() if k in ('Wq', 'bq', 'Wk', 'bk', 'Wv', 'bv', 'Wo', 'bo')}
    del _L0_xattn_all

    def _L0_ffn_setup():
        import jax, jax.numpy as jnp
        import numpy as np
        NUM_EXPERTS = 8
        TOP_K = 2
        B, T, D, F = (4, 256, 128, 352)
        key = jax.random.key(seed)
        ks = jax.random.split(key, 5)
        return {'x': jax.random.normal(ks[0], (B, T, D), dtype=jnp.float32), 'router_w': jax.random.normal(ks[1], (D, NUM_EXPERTS), dtype=jnp.float32) * 0.02, 'gate_proj': jax.random.normal(ks[2], (NUM_EXPERTS, D, F), dtype=jnp.float32) * 0.02, 'up_proj': jax.random.normal(ks[3], (NUM_EXPERTS, D, F), dtype=jnp.float32) * 0.02, 'down_proj': jax.random.normal(ks[4], (NUM_EXPERTS, F, D), dtype=jnp.float32) * 0.02}
    _L0_ffn_all = _L0_ffn_setup()
    _L0_ffn_in = {k: v for k, v in _L0_ffn_all.items() if k in ('router_w', 'gate_proj', 'up_proj', 'down_proj')}
    del _L0_ffn_all
    return {'x': x, 'ctx_1024': ctx_1024, 'L0_attn_Wq': _L0_attn_in['Wq'], 'L0_attn_Wk': _L0_attn_in['Wk'], 'L0_attn_Wv': _L0_attn_in['Wv'], 'L0_attn_Wo': _L0_attn_in['Wo'], 'L0_attn_bo': _L0_attn_in['bo'], 'L0_xattn_Wq': _L0_xattn_in['Wq'], 'L0_xattn_bq': _L0_xattn_in['bq'], 'L0_xattn_Wk': _L0_xattn_in['Wk'], 'L0_xattn_bk': _L0_xattn_in['bk'], 'L0_xattn_Wv': _L0_xattn_in['Wv'], 'L0_xattn_bv': _L0_xattn_in['bv'], 'L0_xattn_Wo': _L0_xattn_in['Wo'], 'L0_xattn_bo': _L0_xattn_in['bo'], 'L0_ffn_router_w': _L0_ffn_in['router_w'], 'L0_ffn_gate_proj': _L0_ffn_in['gate_proj'], 'L0_ffn_up_proj': _L0_ffn_in['up_proj'], 'L0_ffn_down_proj': _L0_ffn_in['down_proj']}

def reference(x, ctx_1024, L0_attn_Wq, L0_attn_Wk, L0_attn_Wv, L0_attn_Wo, L0_attn_bo, L0_xattn_Wq, L0_xattn_bq, L0_xattn_Wk, L0_xattn_bk, L0_xattn_Wv, L0_xattn_bv, L0_xattn_Wo, L0_xattn_bo, L0_ffn_router_w, L0_ffn_gate_proj, L0_ffn_up_proj, L0_ffn_down_proj):
    import jax
    import jax.numpy as jnp

    def _L0_attn_ref(x, Wq, Wk, Wv, Wo, bo):
        import jax, jax.numpy as jnp
        import numpy as np
        B, T, D_MODEL = (4, 512, 128)
        H = 16
        DH = D_MODEL // H
        EPS = 1e-06
        CHUNK = 128

        def _feature(x):
            return jnp.where(x > 0, x + 1.0, jnp.exp(x))

        def _causal_dot_product(Q, K, V):
            b, h, t, d = Q.shape
            nc = t // CHUNK
            mask = jnp.tril(jnp.ones((CHUNK, CHUNK), dtype=Q.dtype))
            qs = jnp.moveaxis(Q.reshape(b, h, nc, CHUNK, d), 2, 0)
            ks = jnp.moveaxis(K.reshape(b, h, nc, CHUNK, d), 2, 0)
            vs = jnp.moveaxis(V.reshape(b, h, nc, CHUNK, d), 2, 0)

            def step(S, qkv):
                q, k, v = qkv
                attn = jnp.einsum('bhid,bhjd->bhij', q, k) * mask
                out = jnp.einsum('bhij,bhjd->bhid', attn, v) + jnp.einsum('bhid,bhde->bhie', q, S)
                S = S + jnp.einsum('bhcd,bhce->bhde', k, v)
                return (S, out)
            S0 = jnp.zeros((b, h, d, d), dtype=Q.dtype)
            _, outs = jax.lax.scan(step, S0, (qs, ks, vs))
            return jnp.moveaxis(outs, 0, 2).reshape(b, h, t, d)
        b, t, _ = x.shape

        def proj(W):
            return (x @ W).reshape(b, t, H, DH).transpose(0, 2, 1, 3)
        Q = _feature(proj(Wq))
        K = _feature(proj(Wk))
        V = proj(Wv)
        Z = 1.0 / (jnp.einsum('bhtd,bhtd->bht', Q, jnp.cumsum(K, axis=1)) + EPS)
        unnorm = _causal_dot_product(Q, K, V)
        out = unnorm * Z[..., None]
        out = out.transpose(0, 2, 1, 3).reshape(b, t, H * DH)
        return out @ Wo + bo

    def _L0_xattn_ref(q, k, v, Wq, bq, Wk, bk, Wv, bv, Wo, bo):
        import jax, jax.numpy as jnp
        import numpy as np
        H = 16
        D = 64
        b, n_q, _ = q.shape
        n_k = k.shape[1]
        qh = (q @ Wq + bq).reshape(b, n_q, H, D)
        kh = (k @ Wk + bk).reshape(b, n_k, H, D)
        vh = (v @ Wv + bv).reshape(b, n_k, H, D)
        scores = jnp.einsum('bnhd,bmhd->bhnm', qh, kh)
        causal = jnp.triu(jnp.ones((n_q, n_k), dtype=bool), k=1)
        scores = jnp.where(causal, -jnp.inf, scores)
        att = jax.nn.softmax(scores / np.sqrt(D).astype(np.float32), axis=-1)
        att_out = jnp.einsum('bhnm,bmhd->bnhd', att, vh).reshape(b, n_q, H * D)
        return att_out @ Wo + bo

    def _L0_ffn_ref(x, router_w, gate_proj, up_proj, down_proj):
        import jax, jax.numpy as jnp
        import numpy as np
        NUM_EXPERTS = 8
        TOP_K = 2
        B, T, D, F = (4, 256, 128, 352)
        scores = jnp.einsum('btd,de->bte', x, router_w).astype(jnp.float32)
        probs = jax.nn.softmax(scores, axis=-1)
        routing_weights, routing_idx = jax.lax.top_k(probs, TOP_K)
        routing_weights = (routing_weights / jnp.sum(routing_weights, axis=-1, keepdims=True)).astype(x.dtype)
        one_hot = jax.nn.one_hot(routing_idx, NUM_EXPERTS, dtype=x.dtype)
        expert_w = jnp.einsum('btke,btk->bte', one_hot, routing_weights)
        dispatched = jnp.einsum('btd,btke->bted', x, one_hot)
        gate = jnp.einsum('bted,edf->btef', dispatched, gate_proj)
        up = jnp.einsum('bted,edf->btef', dispatched, up_proj)
        acts = jax.nn.silu(gate) * up
        expert_out = jnp.einsum('btef,efd->bted', acts, down_proj)
        return jnp.einsum('bted,bte->btd', expert_out, expert_w)
    x = _layernorm(x + _L0_attn_ref(x, L0_attn_Wq, L0_attn_Wk, L0_attn_Wv, L0_attn_Wo, L0_attn_bo), axis=-1)
    x = _layernorm(x + _L0_xattn_ref(x, ctx_1024, ctx_1024, L0_xattn_Wq, L0_xattn_bq, L0_xattn_Wk, L0_xattn_bk, L0_xattn_Wv, L0_xattn_bv, L0_xattn_Wo, L0_xattn_bo), axis=-1)
    x = _layernorm(x + _L0_ffn_ref(x, L0_ffn_router_w, L0_ffn_gate_proj, L0_ffn_up_proj, L0_ffn_down_proj), axis=-1)
    return x

_drawn_inputs = setup_inputs


def setup_inputs(seed=0):
    import zlib

    import numpy as np

    out = dict(_drawn_inputs(seed))
    spreads = {}
    factors = {'L0_attn_Wq': 8.0,
     'L0_attn_bo': 3.656,
     'L0_xattn_bq': 8.0,
     'L0_xattn_bk': 8.0,
     'L0_xattn_bv': 3.878,
     'L0_xattn_bo': 8.0,
     'L0_ffn_router_w': 8.0,
     'L0_ffn_gate_proj': 8.0,
     'L0_ffn_up_proj': 8.0,
     'L0_ffn_down_proj': 8.0}
    for name, (base, spread) in spreads.items():
        noise = np.random.default_rng([zlib.crc32(name.encode()), seed]).standard_normal(out[name].shape)
        drawn = base * np.exp(spread * noise) if base else spread * noise
        out[name] = jnp.asarray(drawn.astype(out[name].dtype))
    for name, factor in factors.items():
        out[name] = (out[name] * factor).astype(out[name].dtype)
    return out
```

```python
from contextlib import ExitStack

import concourse.bass as bass
from concourse import mybir

F32 = mybir.dt.float32
BF16 = mybir.dt.bfloat16
F16 = mybir.dt.float16
I32 = mybir.dt.int32
ALU = mybir.AluOpType
ACT = mybir.ActivationFunctionType
AX = mybir.AxisListType

P = 128
B, T, D = 4, 512, 128
NTOK = B * T
NT = NTOK // P
TPB = T // P
H1, DH = 16, 8
H2, DX, M = 16, 64, 32
HM = H2 * M
BM = B * M
NPAIR = H2 // 2
KT4 = HM // P
E, F = 8, 352
FK = [128, 128, 96]
NF = len(FK)
TOPK = 2
NPK = TOPK * NT
NSLOT = TOPK * NTOK // P + E - 1
UNR = 3
NIT = NSLOT // UNR
EPS_Z = 1e-6
EPS_LN = 1e-5
BIG = 1e30
assert NIT * UNR == NSLOT and sum(FK) == F

C_ID = 0
C_TRI = C_ID + P
C_BLK = C_TRI + P
C_SEG = C_BLK + P
C_REV = C_SEG + P
C_IOTA = C_REV + P
C_ONES = C_IOTA + P
C_J128 = C_ONES + P
C_TOK = C_J128 + NSLOT
C_DUMMY = C_TOK + NPK
C_HALF = C_DUMMY + NSLOT
C_EPS = C_HALF + 16
NCONST = C_EPS + 1
B_ID, B_STRICT, B_ONE, B_MASK = 0, P, 2 * P, 3 * P
NCONSTB = B_MASK + HM

SEMS = """ld_x ld_w1 ld_const ld_constb ld_ctx ld_wkv ld_wq ld_bias ld_wo2 ld_gu ld_dn ld_bo1
 kt_ps vt_ps kt_sb vt_sb g_ps g_sb c_ps c_hi c_r1 c_mid c_r2 c_split csT_ps csT_sb crow_zero crow_ld
 vwt_ps vwt_sb vw_ps vw_sb xb_ready
 qkv_ps er_ready v_ready feat kc_ready kq_ready den_ready dene_ready z_ready kv_ready u_ps qu_ready intra_ready
 s_ps sblk_ready qt_ps qt_sb inter_ps comb_ready out_ready outT_ps oT_sb wo_ps y1_ready st1_ready var1_ready
 ve1_ready rs1_ready x1_ready x1t_ps x1t_sb sc_ps max_ready sd_ready exp_ready sum_ready rsm_ready pn_ready
 pt_ps pt_sb pv_ps y2_ready st2_ready var2_ready ve2_ready rs2_ready x2_ready x2_ld x2t_ps x2t_sb rt_ps
 logits_ready route e2_ready onehot_ready rank_ps rowsel_ready slot_ps idx_ready gathered xgt_ps xgt_sb
 gate_ps up_ps silu_ready a_ready at_ps at_sb down_ps y_ready z_st dl_ready z_var z_ve z_rs zn_ready out_st""".split()


def decoder_layer(nc, xn, xT, wqkv, wo1, bo1, consts, constb, ctxT, wk, wv, wqT, biases, wo2, router,
                  wgu, wdn, out):
    x2_dram = nc.dram_tensor("x2_rows", (NTOK, D), F32, kind="Internal").ap()
    y_dram = nc.dram_tensor("expert_rows", (TOPK * NTOK + NSLOT * P, D), F32, kind="Internal").ap()

    with ExitStack() as ctx:
        def sb(name, shape, dt=F32):
            return ctx.enter_context(nc.sbuf_tensor(name, shape, dt))

        S = {n: ctx.enter_context(nc.semaphore(n)) for n in SEMS}
        xt_loaded = [ctx.enter_context(nc.semaphore(f"xt_loaded{c}")) for c in range(TPB)]
        x2_stored = [ctx.enter_context(nc.semaphore(f"x2_stored{c}")) for c in range(TPB)]
        y_ld = [ctx.enter_context(nc.semaphore(f"y_ld{g}")) for g in range(4)]
        xg_loaded = [ctx.enter_context(nc.semaphore(f"xg_loaded{c}")) for c in range(UNR)]
        y_scattered = [ctx.enter_context(nc.semaphore(f"y_scattered{c}")) for c in range(UNR)]

        c32 = sb("c32", [P, NCONST])
        cb = sb("cb", [P, NCONSTB], BF16)
        wqkv_sb = sb("wqkv_sb", [P, 3 * D])
        wo1_sb = sb("wo1_sb", [P, D])
        bo1_sb = sb("bo1_sb", [P, D])
        router_sb = sb("router_sb", [P, E])
        wgu_sb = sb("wgu_sb", [P, E * 2 * F])
        wdn_sb = sb("wdn_sb", [P, E * NF * D])
        ident, tri = c32[:, C_ID:C_ID + P], c32[:, C_TRI:C_TRI + P]
        blockmask, segment = c32[:, C_BLK:C_BLK + P], c32[:, C_SEG:C_SEG + P]
        identb, strictb, onesb = cb[:, B_ID:B_ID + P], cb[:, B_STRICT:B_STRICT + P], cb[:, B_ONE:B_ONE + P]
        causalb = cb[:, B_MASK:B_MASK + HM]
        ctx_sb = sb("ctx_sb", [P, BM])
        early = sb("early", [P, 8 * H2 * DX])
        part = lambda k, n=1: early[:, k * H2 * DX:(k + n) * H2 * DX]
        wk_sb, wv_sb = part(0), part(1)
        wq_sb = part(2).rearrange("p (q d) -> p q d", q=NPAIR)
        wo2_sb = part(3).rearrange("p (q d) -> p q d", q=NPAIR)
        kT = part(4).rearrange("p (q m) -> p q m", q=NPAIR)
        vT = part(5).rearrange("p (q m) -> p q m", q=NPAIR)
        vwT = part(6, 2).rearrange("p (b m) -> p b m", b=B)
        yk = part(0, 4).rearrange("p (k n d) -> p k n d", k=TOPK, d=D)
        z = part(4, 2).rearrange("p (n d) -> p n d", d=D)
        zn = part(6, 2).rearrange("p (n d) -> p n d", d=D)
        bias_sb = sb("bias_sb", [P, 3 * NPAIR + 1])
        G = sb("G", [P, B, HM])
        VW = sb("VW", [P, B, KT4 * D])
        c_r = sb("c_r", [P, 2, H2])
        c_parts = sb("c_parts", [P, 3, H2], BF16)
        c_partsT = sb("c_partsT", [H2, 3, BM], BF16)
        crow = sb("crow", [P, B, HM], BF16)
        x_all = sb("x_all", [P, NT, D])
        xb_all = sb("xb_all", [P, NT, D])
        xT_sb = sb("xT_sb", [P, TPB, P])
        ex = sb("ex", [P, 2, 2 * D])
        rl = sb("rl", [P, 2, 2 * D])
        vn = sb("vn", [P, 2, D])
        qk = sb("qk", [P, 2, 2 * D])
        kcum = sb("kcum", [P, D])
        kcq = sb("kcq", [P, D])
        den = sb("den", [P, 2, H1])
        Z = sb("Z", [P, 2, H1])
        kv = sb("kv", [P, 2, DH * D])
        qu = sb("qu", [P, DH * D])
        intra = sb("intra", [P, D])
        osum = sb("osum", [P, D])
        on_t = sb("on_t", [P, D])
        sblk = sb("sblk", [P, D])
        qT = sb("qT", [P, P])
        oT = sb("oT", [P, P])
        y1 = sb("y1", [P, 2, D])
        st = sb("st", [P, 2, 6])
        mv1 = sb("mv1", [P, 2, 2])
        ve = sb("ve", [P, 2])
        rs1 = sb("rs1", [P, 2])
        x1 = sb("x1", [P, 2, D])
        x1T = sb("x1T", [P, P])
        mx = sb("mx", [P, H2])
        pr = sb("pr", [P, 2, HM])
        sm = sb("sm", [P, H2])
        rsm = sb("rsm", [P, 2, H2])
        pn = sb("pn", [P, 2, HM])
        pT = sb("pT", [P, HM])
        y2 = sb("y2", [P, 2, D])
        mv2 = sb("mv2", [P, 2, 2])
        rs2 = sb("rs2", [P, 2])
        x2_ring = sb("x2_ring", [P, TPB, D])
        x2_all = sb("x2_all", [P, NT, D])
        x2T = sb("x2T", [P, P])
        logits = sb("logits", [P, NT, E])
        top = sb("top", [P, TOPK, NT])
        eq = sb("eq", [P, NT, E])
        cand = sb("cand", [P, NT, E])
        pick = sb("pick", [P, NT])
        onehot = sb("onehot", [P, TOPK, NT, E])
        l2nd = sb("l2nd", [P, NT, E])
        hotb = sb("hotb", [P, NT, E], BF16)
        dl = sb("dl", [P, NT])
        e2 = sb("e2", [P, NT])
        wtop = sb("wtop", [P, TOPK, NT])
        tot = sb("tot", [P, E, NT])
        cnt = sb("cnt", [P, E])
        cnti = sb("cnti", [P, E], I32)
        pad = sb("pad", [P, E])
        scan = sb("scan", [P, E, NT])
        base = sb("base", [P, E, NT])
        pos = sb("pos", [P, NT, E])
        posk = sb("posk", [P, TOPK, NT, E])
        slot = sb("slot", [P, NPK])
        sloti = sb("sloti", [P, NPK], I32)
        rowi = sb("rowi", [P, 2, NPK], I32)
        rowf = sb("rowf", [P, 2, NPK])
        endcmp = sb("endcmp", [P, NSLOT, E])
        texp = sb("texp", [P, NSLOT])
        texpi = sb("texpi", [P, NSLOT], I32)
        rowsel = sb("rowsel", [P, NPK, P], F16)
        tilesel = sb("tilesel", [P, NPK, NSLOT], F16)
        sv = sb("sv", [P, 4, NSLOT])
        src_row = sb("src_row", [P, NSLOT], I32)
        dst_row = sb("dst_row", [P, NSLOT], I32)
        xg = sb("xg", [P, UNR, D])
        xgT = sb("xgT", [P, UNR, P])
        sg = sb("sg", [P, F])
        act = sb("act", [P, UNR, F])
        aT = sb("aT", [P, UNR, NF * P])
        yx = sb("yx", [P, UNR, D])
        stz = sb("stz", [P, NT, 6])
        mvz = sb("mvz", [P, NT, 2])
        vez = sb("vez", [P, NT])
        rsz = sb("rsz", [P, NT])

        ps = [ctx.enter_context(nc.psum_tensor(f"bank{i}", [P, 512], F32)) for i in range(8)]
        block = ctx.enter_context(nc.Block())

        def tile_steps(eng, step, lag):
            for c in range(TPB):
                step(0, c)
            with eng.Fori(1, B) as b:
                for c in range(TPB):
                    step(b, c)
            for c in range(lag):
                step(B, c)

        def on(b, c, lag):
            return not isinstance(b, int) or 0 <= TPB * b + c - lag < NT

        def cnt_of(b, c, lag):
            return TPB * b + (c - lag + 1)

        def carries(b, c, lag):
            k = c - lag
            return 3 * (b + k // TPB) + k % TPB

        def wait(eng, sem, v):
            if not isinstance(v, int) or v > 0:
                eng.wait_ge(sem, v)

        @block.sync
        def _(sp):
            sp.dma_start(xT_sb[:, 0, :], xT[:, 0:P]).then_inc(xt_loaded[0], 16)
            sp.dma_start(wqkv_sb[:], wqkv).then_inc(S["ld_w1"], 16)
            sp.dma_start(ctx_sb[:], ctxT).then_inc(S["ld_ctx"], 16)
            sp.dma_start(wk_sb, wk).then_inc(S["ld_wkv"], 16)
            sp.dma_start(wv_sb, wv).then_inc(S["ld_wkv"], 16)
            sp.dma_start(bias_sb[:], biases).then_inc(S["ld_bias"], 16)
            sp.dma_start(c32[:], consts).then_inc(S["ld_const"], 16)
            sp.dma_start(wq_sb, wqT).then_inc(S["ld_wq"], 16)
            sp.dma_start(wo2_sb, wo2).then_inc(S["ld_wo2"], 16)
            sp.dma_start(cb[:], constb).then_inc(S["ld_constb"], 16)
            sp.dma_start(x_all[:], xn.rearrange("(n p) d -> p n d", p=P)).then_inc(S["ld_x"], 16)
            sp.dma_start(bo1_sb[:], bo1.partition_broadcast(P)).then_inc(S["ld_bo1"], 16)
            sp.dma_start(wo1_sb[:], wo1).then_inc(S["ld_w1"], 16)
            sp.dma_start(router_sb[:], router).then_inc(S["ld_w1"], 16)
            for c in range(1, TPB):
                sp.dma_start(xT_sb[:, c, :], xT[:, c * P:(c + 1) * P]).then_inc(xt_loaded[c], 16)
            sp.wait_ge(S["csT_sb"], 1)
            sp.wait_ge(S["crow_zero"], 1)
            for k in range(3):
                for b in range(B):
                    sp.dma_start(crow[k:k + 1, b, :].rearrange("o (h m) -> o h m", m=M),
                                 c_partsT[:, k, b * M:(b + 1) * M]).then_inc(S["crow_ld"], 16)
            sp.dma_start(wgu_sb[:], wgu).then_inc(S["ld_gu"], 16)
            sp.dma_start(wdn_sb[:], wdn).then_inc(S["ld_dn"], 16)

            def step(b, c):
                if not isinstance(b, int) or b < B - 1:
                    sp.wait_ge(S["qkv_ps"], cnt_of(b, c, 0))
                    sp.dma_start(xT_sb[:, c, :], xT[:, bass.ds((b + 1) * T + c * P, P)]).then_inc(xt_loaded[c], 16)
                if on(b, c, 4):
                    sp.wait_ge(S["x2_ready"], cnt_of(b, c, 4))
                    sp.dma_start(x2_dram[bass.ds((b - 1) * T + c * P, P), :],
                                 x2_ring[:, c, :]).then_inc(x2_stored[c], 16)

            for c in range(TPB):
                step(0, c)
            with sp.Fori(1, B - 1) as b:
                for c in range(TPB):
                    step(b, c)
            for b in (B - 1, B):
                for c in range(TPB):
                    step(b, c)
            for c in range(TPB):
                sp.wait_ge(x2_stored[c], 16 * (B + 1))
            sp.dma_start(x2_all[:], x2_dram.rearrange("(n p) d -> p n d", p=P)).then_inc(S["x2_ld"], 16)
            for k in range(UNR):
                sp.wait_ge(y_scattered[k], 16 * NIT)
            yv = y_dram[0:TOPK * NTOK, :].rearrange("(k n p) d -> p k n d", p=P, k=TOPK)
            for g in range(4):
                for k in range(TOPK):
                    sp.dma_start(yk[:, k, 4 * g:4 * g + 4, :], yv[:, k, 4 * g:4 * g + 4, :]).then_inc(y_ld[g], 16)
            ov = out.rearrange("(n p) d -> p n d", p=P)
            for g in range(4):
                sp.wait_ge(S["zn_ready"], g + 1)
                sp.dma_start(ov[:, 4 * g:4 * g + 4, :], zn[:, 4 * g:4 * g + 4, :]).then_inc(S["out_st"], 16)
            sp.wait_ge(S["out_st"], 64)

        @block.tensor
        def _(pe):
            mm = nc.tensor.matmul
            pe.wait_ge(S["ld_ctx"], 16)
            pe.wait_ge(S["ld_wkv"], 32)
            for w, bank, done in ((wk_sb, 0, "kt_ps"), (wv_sb, 2, "vt_ps")):
                for q in range(NPAIR):
                    last = mm(ps[bank + q // 4][:, (q % 4) * BM:(q % 4 + 1) * BM], w[:, q * P:(q + 1) * P],
                              ctx_sb[:], start=True, stop=True)
                last.then_inc(S[done], 1)
            pe.wait_ge(S["kt_sb"], 1)
            pe.wait_ge(S["ld_wq"], 16)
            for h in range(H2):
                r = slice(DX * (h // NPAIR), DX * (h // NPAIR) + DX)
                last = mm(ps[4 + h // 4][:, (h % 4) * BM:(h % 4 + 1) * BM], wq_sb[r, h % NPAIR, :], kT[r, h % NPAIR, :],
                          start=True, stop=True)
                if h % 4 == 3:
                    last.then_inc(S["g_ps"], 1)
            for h in range(H2):
                r = slice(DX * (h // NPAIR), DX * (h // NPAIR) + DX)
                last = mm(ps[h // NPAIR][:, h % NPAIR:h % NPAIR + 1], kT[r, h % NPAIR, :],
                          bias_sb[r, 2 * NPAIR + h % NPAIR:2 * NPAIR + h % NPAIR + 1],
                          start=True, stop=True)
            last.then_inc(S["c_ps"], 1)
            pe.wait_ge(S["vt_sb"], 1)
            pe.wait_ge(S["ld_wo2"], 16)
            for h in range(H2):
                r = slice(DX * (h // NPAIR), DX * (h // NPAIR) + DX)
                if h % 4 == 0:
                    pe.wait_ge(S["g_sb"], h // 4 + 1)
                last = mm(ps[4 + h // 4][:, (h % 4) * BM:(h % 4 + 1) * BM], wo2_sb[r, h % NPAIR, :], vT[r, h % NPAIR, :],
                          start=True, stop=True)
                if h % 4 == 3:
                    last.then_inc(S["vwt_ps"], 1)
            pe.wait_ge(S["c_split"], 1)
            pe.wait_ge(S["ld_constb"], 16)
            for k in range(3):
                last = nc.tensor.transpose(ps[2].bitcast(BF16)[0:H2, k * BM:(k + 1) * BM], c_parts[:, k, :], identb)
            last.then_inc(S["csT_ps"], 1)
            pe.wait_ge(S["vwt_sb"], 4)
            pe.wait_ge(S["ld_const"], 16)
            for b in range(B):
                for k in range(KT4):
                    last = nc.tensor.transpose(ps[4 + b][:, k * D:(k + 1) * D], vwT[:, b, k * P:(k + 1) * P], ident)
                last.then_inc(S["vw_ps"], 1)

            def step(b, c):
                n = lambda lag: cnt_of(b, c, lag)
                if on(b, c, 2):
                    pe.wait_ge(S["out_ready"], n(2))
                    nc.tensor.transpose(ps[4][:, 0:P], on_t[:], ident).then_inc(S["outT_ps"], 1)
                if on(b, c, 0):
                    pe.wait_ge(xt_loaded[c], 16 * (b + 1))
                    wait(pe, S["v_ready"], n(1))
                    mm(ps[0][:, 0:3 * D], xT_sb[:, c, :], wqkv_sb[:], start=True, stop=True).then_inc(S["qkv_ps"], 1)
                if on(b, c, 2):
                    pe.wait_ge(S["oT_sb"], n(2))
                    mm(ps[4][:, P:P + D], oT[:], wo1_sb[:], start=True, stop=True).then_inc(S["wo_ps"], 1)
                if on(b, c, 3):
                    pe.wait_ge(S["pn_ready"], n(3))
                    wait(pe, S["pt_sb"], n(4))
                    s2 = (c - 3) % 2
                    for k in range(KT4):
                        last = nc.tensor.transpose(ps[6][:, k * P:(k + 1) * P], pn[:, s2, k * P:(k + 1) * P], ident)
                    last.then_inc(S["pt_ps"], 1)
                if on(b, c, 4):
                    pe.wait_ge(S["x2_ready"], n(4))
                    nc.tensor.transpose(ps[7][:, 0:P], x2_ring[:, c, :], ident).then_inc(S["x2t_ps"], 1)
                if on(b, c, 1) and (c - 1) % TPB:
                    pe.wait_ge(S["feat"], n(1))
                    wait(pe, S["y1_ready"], n(2))
                    nc.tensor.transpose(ps[4][:, 2 * P:3 * P], qk[:, (c - 1) % 2, 0:D], ident).then_inc(S["qt_ps"], 1)
                if on(b, c, 1):
                    s2 = (c - 1) % 2
                    pe.wait_ge(S["kv_ready"], n(1))
                    wait(pe, S["qu_ready"], n(2))
                    for k in range(2):
                        last = mm(ps[1 + k][:], tri, kv[:, s2, k * 512:(k + 1) * 512], start=True, stop=True)
                    last.then_inc(S["u_ps"], 1)
                    if (c - 1) % TPB < TPB - 1:
                        wait(pe, S["sblk_ready"], carries(b, c, 1))
                        mm(ps[3][:, 0:D], qk[:, s2, D:2 * D], vn[:, s2, :], start=(c - 1) % TPB == 0, stop=True,
                           skip_group_check=True).then_inc(S["s_ps"], 1)
                if on(b, c, 4):
                    pe.wait_ge(S["x2t_sb"], n(4))
                    mm(ps[7][:, P:P + E], x2T[:], router_sb[:], start=True, stop=True).then_inc(S["rt_ps"], 1)
                if on(b, c, 3):
                    pe.wait_ge(S["pt_sb"], n(3))
                    wait(pe, S["logits_ready"], n(4))
                    bb = b + (c - 3) // TPB
                    for k in range(KT4):
                        last = mm(ps[7][:, 256:256 + D], pT[:, k * P:(k + 1) * P], VW[:, bb, k * D:(k + 1) * D]
                                  if isinstance(bb, int) else VW[:, bass.ds(bb, 1), k * D:(k + 1) * D],
                                  start=k == 0, stop=k == KT4 - 1)
                    last.then_inc(S["pv_ps"], 1)
                if on(b, c, 2):
                    pe.wait_ge(S["x1_ready"], n(2))
                    if on(b, c, 1):
                        wait(pe, S["qt_sb"], carries(b, c, 1))
                    nc.tensor.transpose(ps[4][:, 0:P], x1[:, (c - 2) % 2, :], ident).then_inc(S["x1t_ps"], 1)
                if on(b, c, 1) and (c - 1) % TPB:
                    pe.wait_ge(S["qt_sb"], carries(b, c, 1))
                    pe.wait_ge(S["sblk_ready"], carries(b, c, 1))
                    wait(pe, S["x1t_sb"], n(2))
                    mm(ps[4][:, 3 * P:3 * P + D], qT[:], sblk[:], start=True, stop=True).then_inc(S["inter_ps"], 1)
                if on(b, c, 2):
                    pe.wait_ge(S["x1t_sb"], n(2))
                    wait(pe, S["sd_ready"], n(3))
                    bb = b + (c - 2) // TPB
                    first = (c - 2) % TPB == 0
                    row = lambda t: t[:, bb, :] if isinstance(bb, int) else t[:, bass.ds(bb, 1), :]
                    mm(ps[5][:], x1T[:], row(G), start=True, stop=False)
                    last = mm(ps[5][:], onesb, row(crow), start=False, stop=not first)
                    if first:
                        last = mm(ps[5][:], identb, causalb, start=False, stop=True)
                    last.then_inc(S["sc_ps"], 1)

            pe.wait_ge(S["crow_ld"], 3 * B * 16)
            pe.wait_ge(S["vw_sb"], 4)
            pe.wait_ge(S["ld_w1"], 48)
            tile_steps(pe, step, 4)

            pe.wait_ge(S["onehot_ready"], 1)
            hb = hotb[:].rearrange("p n e -> p (n e)")
            mm(ps[0][:, 0:P], strictb, hb, start=True, stop=True)
            mm(ps[0][:, P:2 * P], onesb, hb, start=True, stop=True).then_inc(S["rank_ps"], 1)
            for i in range(NPK):
                if i % 8 == 0:
                    pe.wait_ge(S["rowsel_ready"], i // 8 + 1)
                last = mm(ps[1][:, 0:NSLOT], rowsel[:, i, :], tilesel[:, i, :], start=i == 0, stop=i == NPK - 1)
            last.then_inc(S["slot_ps"], 1)
            pe.wait_ge(S["idx_ready"], 1)
            pe.wait_ge(S["ld_gu"], 16)
            pe.wait_ge(S["ld_dn"], 16)

            def estep(i, u):
                has = lambda lag: not isinstance(i, int) or 0 <= UNR * i + u - lag < NSLOT
                n = lambda lag: UNR * i + (u - lag + 1)
                sl = lambda lag: (u - lag) % UNR
                expert = lambda lag: pe.value_load(texpi[0:1, bass.ds(UNR * i + (u - lag), 1)], min_val=0, max_val=E - 1)
                if has(1):
                    e = expert(1)
                    pe.wait_ge(S["xgt_sb"], n(1))
                    wait(pe, S["silu_ready"], n(2))
                    mm(ps[0][:, 0:F], xgT[:, sl(1), :], wgu_sb[:, bass.ds(e * (2 * F), F)], start=True,
                       stop=True).then_inc(S["gate_ps"], 1)
                if has(3):
                    ed = expert(3)
                    pe.wait_ge(S["at_sb"], n(3))
                    wait(pe, S["y_ready"], n(4))
                    for k, f in enumerate(FK):
                        last = mm(ps[3][:, 0:D], aT[0:f, sl(3), k * P:(k + 1) * P],
                                  wdn_sb[0:f, bass.ds(ed * (NF * D) + k * D, D)], start=k == 0, stop=k == NF - 1)
                    last.then_inc(S["down_ps"], 1)
                if has(1):
                    wait(pe, S["a_ready"], n(2))
                    mm(ps[1][:, 0:F], xgT[:, sl(1), :], wgu_sb[:, bass.ds(e * (2 * F) + F, F)], start=True,
                       stop=True).then_inc(S["up_ps"], 1)
                if has(2):
                    pe.wait_ge(S["a_ready"], n(2))
                    wait(pe, S["at_sb"], n(3))
                    for k, f in enumerate(FK):
                        last = nc.tensor.transpose(ps[2][0:f, k * P:(k + 1) * P], act[:, sl(2), k * P:k * P + f], ident)
                    last.then_inc(S["at_ps"], 1)
                if has(0):
                    pe.wait_ge(xg_loaded[u], 16 * (i + 1))
                    wait(pe, S["xgt_sb"], n(1))
                    nc.tensor.transpose(ps[4][:, 0:P], xg[:, u, :], ident).then_inc(S["xgt_ps"], 1)

            for i in range(2):
                for u in range(UNR):
                    estep(i, u)
            with pe.Fori(2, NIT) as i:
                for u in range(UNR):
                    estep(i, u)
            for u in range(3):
                estep(NIT, u)

        @block.scalar
        def _(ac):
            act_f = nc.scalar.activation
            for g in range(4):
                ac.wait_ge(S["g_ps"], g + 1)
                act_f(G[:, :, g * P:(g + 1) * P].rearrange("p b (h m) -> p h b m", m=M),
                      ps[4 + g][:].rearrange("p (h b m) -> p h b m", b=B, m=M), ACT.Copy).then_inc(S["g_sb"], 1)
            ac.wait_ge(S["csT_ps"], 1)
            act_f(c_partsT[:].rearrange("p k m -> p (k m)"), ps[2].bitcast(BF16)[0:H2, 0:3 * BM], ACT.Copy).then_inc(S["csT_sb"], 1)
            for b in range(B):
                ac.wait_ge(S["vw_ps"], b + 1)
                act_f(VW[:, b, :], ps[4 + b][:], ACT.Copy).then_inc(S["vw_sb"], 1)

            def step(b, c):
                n = lambda lag: cnt_of(b, c, lag)
                if on(b, c, 2):
                    ac.wait_ge(S["outT_ps"], n(2))
                    act_f(oT[:], ps[4][:, 0:P], ACT.Copy).then_inc(S["oT_sb"], 1)
                if on(b, c, 0):
                    s2 = c % 2
                    ac.wait_ge(S["qkv_ps"], n(0))
                    wait(ac, S["feat"], n(2))
                    wait(ac, S["kv_ready"], n(2))
                    act_f(ex[:, s2, :], ps[0][:, 0:2 * D], ACT.Exp)
                    act_f(rl[:, s2, :], ps[0][:, 0:2 * D], ACT.Relu).then_inc(S["er_ready"], 1)
                    act_f(vn[:, s2, :], ps[0][:, 2 * D:3 * D], ACT.Copy).then_inc(S["v_ready"], 1)
                if on(b, c, 3):
                    ac.wait_ge(S["pt_ps"], n(3))
                    act_f(pT[:], ps[6][:], ACT.Copy).then_inc(S["pt_sb"], 1)
                if on(b, c, 4):
                    ac.wait_ge(S["x2t_ps"], n(4))
                    act_f(x2T[:], ps[7][:, 0:P], ACT.Copy).then_inc(S["x2t_sb"], 1)
                if on(b, c, 1) and (c - 1) % TPB:
                    ac.wait_ge(S["qt_ps"], carries(b, c, 1))
                    act_f(qT[:], ps[4][:, 2 * P:3 * P], ACT.Copy).then_inc(S["qt_sb"], 1)
                if on(b, c, 2):
                    ac.wait_ge(S["x1t_ps"], n(2))
                    act_f(x1T[:], ps[4][:, 0:P], ACT.Copy).then_inc(S["x1t_sb"], 1)
                    ac.wait_ge(S["sd_ready"], n(2))
                    act_f(pr[:, (c - 2) % 2, :], pr[:, (c - 2) % 2, :], ACT.Exp,
                          scale=float(DX) ** -0.5).then_inc(S["exp_ready"], 1)

            tile_steps(ac, step, 4)
            ac.wait_ge(S["dl_ready"], 1)
            act_f(e2[:], dl[:], ACT.Exp).then_inc(S["e2_ready"], 1)

            def estep(i, u):
                has = lambda lag: not isinstance(i, int) or 0 <= UNR * i + u - lag < NSLOT
                n = lambda lag: UNR * i + (u - lag + 1)
                if has(1):
                    ac.wait_ge(S["gate_ps"], n(1))
                    wait(ac, S["a_ready"], n(2))
                    act_f(sg[:], ps[0][:, 0:F], ACT.Silu).then_inc(S["silu_ready"], 1)
                if has(2):
                    ac.wait_ge(S["at_ps"], n(2))
                    wait(ac, S["down_ps"], UNR * i + (u - 2) - UNR + 1)
                    for lo, hi, f in ((0, 2 * P, P), (2 * P, 3 * P, FK[2])):
                        last = act_f(aT[0:f, (u - 2) % UNR, lo:hi], ps[2][0:f, lo:hi], ACT.Copy)
                    last.then_inc(S["at_sb"], 1)
                if has(0):
                    ac.wait_ge(S["xgt_ps"], n(0))
                    wait(ac, S["up_ps"], UNR * i + u - UNR + 1)
                    act_f(xgT[:, u, :], ps[4][:, 0:P], ACT.Copy).then_inc(S["xgt_sb"], 1)

            for i in range(2):
                for u in range(UNR):
                    estep(i, u)
            with ac.Fori(2, NIT) as i:
                for u in range(UNR):
                    estep(i, u)
            for u in range(3):
                estep(NIT, u)

        @block.gpsimd
        def _(pool):
            g = nc.gpsimd
            g.memset(crow[:], 0.0).then_inc(S["crow_zero"], 1)
            pool.wait_ge(S["ld_x"], 16)
            pool.wait_ge(S["ld_bo1"], 16)
            g.tensor_tensor(xb_all[:], x_all[:], bo1_sb[:].unsqueeze(1).broadcast_to([P, NT, D]),
                            ALU.add).then_inc(S["xb_ready"], 1)
            pool.wait_ge(S["ld_const"], 16)
            half = c32[:, C_HALF:C_HALF + 1]
            eps = c32[:, C_EPS:C_EPS + 1]

            def step(b, c):
                n = lambda lag: cnt_of(b, c, lag)
                if on(b, c, 3):
                    s2 = (c - 3) % 2
                    pool.wait_ge(S["rsm_ready"], n(3))
                    wait(pool, S["pt_ps"], n(4))
                    g.tensor_tensor(pn[:, s2, :].rearrange("p (h m) -> p h m", m=M),
                                    pr[:, s2, :].rearrange("p (h m) -> p h m", m=M),
                                    rsm[:, s2, :].unsqueeze(2).broadcast_to([P, H2, M]), ALU.mult).then_inc(S["pn_ready"], 1)
                if on(b, c, 2):
                    s2 = (c - 2) % 2
                    pool.wait_ge(S["var1_ready"], n(2))
                    g.tensor_tensor(ve[:, 0:1], mv1[:, s2, 1:2], eps, ALU.add).then_inc(S["ve1_ready"], 1)
                    pool.wait_ge(S["ve1_ready"], n(2))
                    g.tensor_tensor(rs1[:, s2:s2 + 1], ve[:, 0:1], half, ALU.pow).then_inc(S["rs1_ready"], 1)
                if on(b, c, 0):
                    s2 = c % 2
                    pool.wait_ge(S["feat"], n(0))
                    pool.wait_ge(S["v_ready"], n(0))
                    wait(pool, S["u_ps"], n(2))
                    g.tensor_tensor(kv[:, s2, :].rearrange("p (d h e) -> p d h e", d=DH, e=DH),
                                    qk[:, s2, D:2 * D].rearrange("p (d h) -> p d h", d=DH).unsqueeze(3)
                                    .broadcast_to([P, DH, H1, DH]),
                                    vn[:, s2, :].rearrange("p (h e) -> p h e", e=DH).unsqueeze(1)
                                    .broadcast_to([P, DH, H1, DH]), ALU.mult).then_inc(S["kv_ready"], 1)
                if on(b, c, 3):
                    s2 = (c - 3) % 2
                    pool.wait_ge(S["var2_ready"], n(3))
                    g.tensor_tensor(ve[:, 1:2], mv2[:, s2, 1:2], eps, ALU.add).then_inc(S["ve2_ready"], 1)
                    pool.wait_ge(S["ve2_ready"], n(3))
                    g.tensor_tensor(rs2[:, s2:s2 + 1], ve[:, 1:2], half, ALU.pow).then_inc(S["rs2_ready"], 1)

            tile_steps(pool, step, 4)

            pool.wait_ge(S["idx_ready"], 1)
            for c in range(TPB):
                pool.wait_ge(x2_stored[c], 16 * (B + 1))
            for j in range(NSLOT + 6):
                if 0 <= j - 6:
                    t = j - 6
                    pool.wait_ge(S["y_ready"], t + 1)
                    g.indirect_dma_start(y_dram, bass.IndirectOffsetOnAxis(ap=dst_row[:, t:t + 1], axis=0),
                                         yx[:, t % UNR, :], None).then_inc(y_scattered[t % UNR], 16)
                if j < NSLOT:
                    if j >= UNR:
                        pool.wait_ge(S["xgt_ps"], j - UNR + 1)
                    g.indirect_dma_start(xg[:, j % UNR, :], None, x2_dram,
                                         bass.IndirectOffsetOnAxis(ap=src_row[:, j:j + 1], axis=0)
                                         ).then_inc(xg_loaded[j % UNR], 16)
            for q in range(4):
                pool.wait_ge(S["z_var"], q + 1)
                sl = slice(4 * q, 4 * q + 4)
                g.tensor_tensor(vez[:, sl], mvz[:, sl, 1], eps.broadcast_to([P, 4]), ALU.add).then_inc(S["z_ve"], 1)
                pool.wait_ge(S["z_ve"], q + 1)
                g.tensor_tensor(rsz[:, sl], vez[:, sl], c32[:, C_HALF:C_HALF + 4], ALU.pow).then_inc(S["z_rs"], 1)

        @block.vector
        def _(dv):
            v = nc.vector
            TT, TS, STT = v.tensor_tensor, v.tensor_scalar, v.scalar_tensor_tensor
            dv.wait_ge(S["ld_bias"], 16)
            for t, bank, col, src, done in ((kT, 0, 0, "kt_ps", "kt_sb"), (vT, 2, NPAIR, "vt_ps", "vt_sb")):
                dv.wait_ge(S[src], 1)
                for k in range(2):
                    last = TT(t[:, 4 * k:4 * k + 4, :], ps[bank + k][:].rearrange("p (q m) -> p q m", q=4),
                              bias_sb[:, col + 4 * k:col + 4 * k + 4].unsqueeze(2).broadcast_to([P, 4, BM]), ALU.add)
                last.then_inc(S[done], 1)
            dv.wait_ge(S["c_ps"], 1)
            for g in range(2):
                hs = slice(g * NPAIR, g * NPAIR + NPAIR)
                last = v.tensor_copy(c_parts[:, 0, hs], ps[g][:, 0:NPAIR])
            last.then_inc(S["c_hi"], 1)
            dv.wait_ge(S["c_hi"], 1)
            for g in range(2):
                hs = slice(g * NPAIR, g * NPAIR + NPAIR)
                last = TT(c_r[:, 0, hs], ps[g][:, 0:NPAIR], c_parts[:, 0, hs], ALU.subtract)
            last.then_inc(S["c_r1"], 1)
            dv.wait_ge(S["c_r1"], 1)
            v.tensor_copy(c_parts[:, 1, :], c_r[:, 0, :]).then_inc(S["c_mid"], 1)
            dv.wait_ge(S["c_mid"], 1)
            TT(c_r[:, 1, :], c_r[:, 0, :], c_parts[:, 1, :], ALU.subtract).then_inc(S["c_r2"], 1)
            dv.wait_ge(S["c_r2"], 1)
            v.tensor_copy(c_parts[:, 2, :], c_r[:, 1, :]).then_inc(S["c_split"], 1)
            for k in range(4):
                dv.wait_ge(S["vwt_ps"], k + 1)
                src = ps[4 + k][:].rearrange("p (h b m) -> p h b m", b=B, m=M)
                dst = vwT[:, :, k * P:(k + 1) * P].rearrange("p b (h m) -> p h b m", m=M)
                if k == 0:
                    TS(dst[:, 0], src[:, 0], bias_sb[:, 3 * NPAIR:3 * NPAIR + 1], None, ALU.add)
                    v.tensor_copy(dst[:, 1:4], src[:, 1:4]).then_inc(S["vwt_sb"], 1)
                else:
                    v.tensor_copy(dst, src).then_inc(S["vwt_sb"], 1)
            dv.wait_ge(S["xb_ready"], 1)
            dv.wait_ge(S["ld_const"], 16)
            for c in range(TPB):
                dv.sem_inc(x2_stored[c], 16)

            def step(b, c):
                n = lambda lag: cnt_of(b, c, lag)
                tile = lambda t, lag: t[:, bass.ds(TPB * b + (c - lag), 1), :]
                if on(b, c, 3):
                    s2 = (c - 3) % 2
                    dv.wait_ge(S["exp_ready"], n(3))
                    v.tensor_reduce(sm[:], pr[:, s2, :].rearrange("p (h m) -> p h m", m=M), AX.X, ALU.add).then_inc(S["sum_ready"], 1)
                    dv.wait_ge(S["sum_ready"], n(3))
                    wait(dv, S["pn_ready"], n(4))
                    v.reciprocal(rsm[:, s2, :], sm[:]).then_inc(S["rsm_ready"], 1)
                if on(b, c, 2):
                    s2 = (c - 2) % 2
                    dv.wait_ge(S["wo_ps"], n(2))
                    TT(y1[:, s2, :].unsqueeze(1), ps[4][:, P:P + D].unsqueeze(1), tile(xb_all, 2), ALU.add).then_inc(S["y1_ready"], 1)
                    dv.wait_ge(S["y1_ready"], n(2))
                    v.bn_stats(st[:, 0, :], y1[:, s2, :]).then_inc(S["st1_ready"], 1)
                    dv.wait_ge(S["st1_ready"], n(2))
                if on(b, c, 0):
                    s2 = c % 2
                    dv.wait_ge(S["er_ready"], n(0))
                    wait(dv, S["kv_ready"], n(2))
                    STT(qk[:, s2, :], ex[:, s2, :], 1.0, rl[:, s2, :], ALU.min, ALU.add).then_inc(S["feat"], 1)
                if on(b, c, 2):
                    v.bn_aggr(mv1[:, (c - 2) % 2, :], st[:, 0, :]).then_inc(S["var1_ready"], 1)
                if on(b, c, 0):
                    s2 = c % 2
                    dv.wait_ge(S["feat"], n(0))
                    v.tensor_tensor_scan(kcum[:], segment, qk[:, s2, D:2 * D], 0.0, ALU.mult, ALU.add).then_inc(S["kc_ready"], 1)
                    dv.wait_ge(S["kc_ready"], n(0))
                    TT(kcq[:], kcum[:], qk[:, s2, 0:D], ALU.mult).then_inc(S["kq_ready"], 1)
                    dv.wait_ge(S["kq_ready"], n(0))
                    v.tensor_reduce(den[:, 0, :], kcq[:].rearrange("p (d h) -> p h d", d=DH), AX.X, ALU.add).then_inc(S["den_ready"], 1)
                    dv.wait_ge(S["den_ready"], n(0))
                    TS(den[:, 1, :], den[:, 0, :], EPS_Z, None, ALU.add).then_inc(S["dene_ready"], 1)
                    dv.wait_ge(S["dene_ready"], n(0))
                    v.reciprocal(Z[:, s2, :], den[:, 1, :]).then_inc(S["z_ready"], 1)
                if on(b, c, 2):
                    s2 = (c - 2) % 2
                    dv.wait_ge(S["rs1_ready"], n(2))
                    TS(x1[:, s2, :], y1[:, s2, :], mv1[:, s2, 0:1], rs1[:, s2:s2 + 1], ALU.subtract, ALU.mult).then_inc(S["x1_ready"], 1)
                if on(b, c, 1):
                    s2 = (c - 1) % 2
                    dv.wait_ge(S["u_ps"], n(1))
                    for k in range(2):
                        last = TT(qu[:, 512 * k:512 * k + 512].rearrange("p (a e) -> p a e", e=DH),
                                  ps[1 + k][:].rearrange("p (a e) -> p a e", e=DH),
                                  qk[:, s2, 64 * k:64 * k + 64].unsqueeze(2).broadcast_to([P, 64, DH]), ALU.mult)
                    last.then_inc(S["qu_ready"], 1)
                    dv.wait_ge(S["qu_ready"], n(1))
                    v.tensor_reduce(intra[:], qu[:].rearrange("p (d f) -> p f d", d=DH), AX.X, ALU.add).then_inc(S["intra_ready"], 1)
                if on(b, c, 4):
                    dv.wait_ge(S["rt_ps"], n(4))
                    v.tensor_copy(tile(logits, 4), ps[7][:, P:P + E].unsqueeze(1)).then_inc(S["logits_ready"], 1)
                if on(b, c, 3):
                    s2 = (c - 3) % 2
                    dv.wait_ge(S["pv_ps"], n(3))
                    TT(y2[:, s2, :], ps[7][:, 256:256 + D], x1[:, s2, :], ALU.add).then_inc(S["y2_ready"], 1)
                    dv.wait_ge(S["y2_ready"], n(3))
                    v.bn_stats(st[:, 1, :], y2[:, s2, :]).then_inc(S["st2_ready"], 1)
                    dv.wait_ge(S["st2_ready"], n(3))
                def aggregate2():
                    if on(b, c, 3):
                        v.bn_aggr(mv2[:, (c - 3) % 2, :], st[:, 1, :]).then_inc(S["var2_ready"], 1)

                if not on(b, c, 1):
                    aggregate2()
                if on(b, c, 1):
                    s2 = (c - 1) % 2
                    zb = Z[:, s2, :].unsqueeze(2).broadcast_to([P, H1, DH])
                    o3 = on_t[:].rearrange("p (h e) -> p h e", e=DH)
                    if (c - 1) % TPB:
                        dv.wait_ge(S["inter_ps"], carries(b, c, 1))
                        dv.wait_ge(S["intra_ready"], n(1))
                        TT(osum[:], ps[4][:, 3 * P:3 * P + D], intra[:], ALU.add).then_inc(S["comb_ready"], 1)
                        aggregate2()
                        dv.wait_ge(S["comb_ready"], carries(b, c, 1))
                        TT(o3, osum[:].rearrange("p (h e) -> p h e", e=DH), zb, ALU.mult).then_inc(S["out_ready"], 1)
                    else:
                        dv.wait_ge(S["intra_ready"], n(1))
                        TT(o3, intra[:].rearrange("p (h e) -> p h e", e=DH), zb, ALU.mult).then_inc(S["out_ready"], 1)
                        aggregate2()
                    if (c - 1) % TPB < TPB - 1:
                        dv.wait_ge(S["s_ps"], carries(b, c, 1) + 1)
                        TT(sblk[:], ps[3][:, 0:D], blockmask, ALU.mult).then_inc(S["sblk_ready"], 1)
                if on(b, c, 3):
                    s2 = (c - 3) % 2
                    dv.wait_ge(S["rs2_ready"], n(3))
                    dv.wait_ge(x2_stored[(c - 3) % TPB], 16 * (b + (c - 3) // TPB + 1))
                    TS(x2_ring[:, (c - 3) % TPB, :], y2[:, s2, :], mv2[:, s2, 0:1], rs2[:, s2:s2 + 1], ALU.subtract,
                       ALU.mult).then_inc(S["x2_ready"], 1)
                if on(b, c, 2):
                    s2 = (c - 2) % 2
                    s3 = ps[5][:].rearrange("p (h m) -> p h m", m=M)
                    dv.wait_ge(S["sc_ps"], n(2))
                    v.tensor_reduce(mx[:], s3, AX.X, ALU.max).then_inc(S["max_ready"], 1)
                    dv.wait_ge(S["max_ready"], n(2))
                    wait(dv, S["pn_ready"], n(4))
                    TT(pr[:, s2, :].rearrange("p (h m) -> p h m", m=M), s3,
                       mx[:].unsqueeze(2).broadcast_to([P, H2, M]), ALU.subtract).then_inc(S["sd_ready"], 1)

            tile_steps(dv, step, 4)

            count = [0]

            def then(ins):
                count[0] += 1
                ins.then_inc(S["route"], 1)
                dv.wait_ge(S["route"], count[0])

            dv.wait_ge(S["logits_ready"], NT)
            rev = c32[:, C_REV:C_REV + P].rearrange("p (n e) -> p n e", e=E)
            lane = lambda t: t.unsqueeze(2).broadcast_to([P, NT, E])
            for k in range(TOPK):
                src = logits if k == 0 else l2nd
                then(v.tensor_reduce(top[:, k, :], src[:], AX.X, ALU.max))
                then(TT(eq[:], src[:], lane(top[:, k, :]), ALU.is_equal))
                then(TT(cand[:], eq[:], rev, ALU.mult))
                then(v.tensor_reduce(pick[:], cand[:], AX.X, ALU.max))
                then(TT(onehot[:, k], rev, lane(pick[:]), ALU.is_equal))
                if k == 0:
                    then(STT(l2nd[:], onehot[:, 0], -3e38, logits[:], ALU.mult, ALU.add))
            TT(hotb[:], onehot[:, 0], onehot[:, 1], ALU.add).then_inc(S["onehot_ready"], 1)
            TT(dl[:], top[:, 1, :], top[:, 0, :], ALU.subtract).then_inc(S["dl_ready"], 1)
            dv.wait_ge(S["e2_ready"], 1)
            then(TS(wtop[:, 1, :], e2[:], 1.0, None, ALU.add))
            then(v.reciprocal(wtop[:, 0, :], wtop[:, 1, :]))
            then(TT(wtop[:, 1, :], wtop[:, 0, :], e2[:], ALU.mult))
            dv.wait_ge(S["rank_ps"], 1)
            then(v.tensor_copy(tot[:], ps[0][:, P:2 * P].rearrange("p (n e) -> p e n", e=E)))
            then(v.tensor_reduce(cnt[:], tot[:], AX.X, ALU.add))
            then(TS(cnti[:], cnt[:], float(P - 1), None, ALU.add))
            then(TS(cnti[:], cnti[:], ~(P - 1), None, ALU.bitwise_and))
            then(TT(pad[:], cnti[:], cnt[:], ALU.subtract))
            then(TT(tot[:, :, NT - 1], tot[:, :, NT - 1], pad[:], ALU.add))
            ones_row = c32[:, C_ONES:C_ONES + P]
            flat = lambda t: t[:].rearrange("p e n -> p (e n)")
            then(v.tensor_tensor_scan(flat(scan), ones_row, flat(tot), 0.0, ALU.mult, ALU.add))
            then(TT(base[:], scan[:], tot[:], ALU.subtract))
            then(TT(pos[:], ps[0][:, 0:P].rearrange("p (n e) -> p n e", e=E), base[:].rearrange("p e n -> p n e"), ALU.add))
            for k in range(TOPK):
                then(TT(posk[:, k], onehot[:, k], pos[:], ALU.mult))
            then(v.tensor_reduce(slot[:], posk[:].rearrange("p k n e -> p (k n) e"), AX.X, ALU.add))
            then(v.tensor_copy(sloti[:], slot[:]))
            then(TS(rowi[:, 0, :], sloti[:], P - 1, None, ALU.bitwise_and))
            then(TS(rowi[:, 1, :], sloti[:], P.bit_length() - 1, None, ALU.logical_shift_right))
            then(v.tensor_copy(rowf[:], rowi[:]))
            iota = c32[:, C_IOTA:C_IOTA + P]
            token = c32[:, C_TOK:C_TOK + NPK]
            for i in range(NPK):
                TS(rowsel[:, i, :], iota, rowf[:, 0, i:i + 1], None, ALU.is_equal)
                last = TS(tilesel[:, i, :], iota[:, 0:NSLOT], rowf[:, 1, i:i + 1], token[:, i:i + 1], ALU.is_equal, ALU.mult)
                if i % 8 == 7:
                    last.then_inc(S["rowsel_ready"], 1)
            then(TT(endcmp[:], c32[:, C_J128:C_J128 + NSLOT].unsqueeze(2).broadcast_to([P, NSLOT, E]),
                    scan[:, :, NT - 1].unsqueeze(1).broadcast_to([P, NSLOT, E]), ALU.is_ge))
            then(v.tensor_reduce(texp[:], endcmp[:], AX.X, ALU.add))
            then(TS(texpi[:], texp[:], float(E - 1), None, ALU.min))
            dv.wait_ge(S["slot_ps"], 1)
            then(v.tensor_copy(sv[:, 0, :], ps[1][:, 0:NSLOT]))
            then(STT(sv[:, 2, :], sv[:, 0, :], -1.0, sv[:, 0, :], ALU.mult, ALU.max))
            then(TS(sv[:, 1, :], sv[:, 2, :], 1.0, -1.0, ALU.max, ALU.add))
            then(v.tensor_copy(src_row[:], sv[:, 1, :]))
            then(TS(sv[:, 2, :], sv[:, 0, :], 0.0, float(NTOK), ALU.is_lt, ALU.mult))
            then(TT(sv[:, 1, :], sv[:, 1, :], sv[:, 2, :], ALU.add))
            then(STT(sv[:, 3, :], sv[:, 0, :], 0.0, c32[:, C_DUMMY:C_DUMMY + NSLOT], ALU.is_equal, ALU.mult))
            TT(dst_row[:], sv[:, 1, :], sv[:, 3, :], ALU.add).then_inc(S["idx_ready"], 1)

            def estep(i, u):
                has = lambda lag: not isinstance(i, int) or 0 <= UNR * i + u - lag < NSLOT
                n = lambda lag: UNR * i + (u - lag + 1)
                if has(3):
                    dv.wait_ge(S["down_ps"], n(3))
                    wait(dv, y_scattered[u], 16 * (i - 1))
                    v.tensor_copy(yx[:, u, :], ps[3][:, 0:D]).then_inc(S["y_ready"], 1)
                if has(1):
                    dv.wait_ge(S["silu_ready"], n(1))
                    dv.wait_ge(S["up_ps"], n(1))
                    wait(dv, S["at_ps"], UNR * i + (u - 1) - UNR + 1)
                    TT(act[:, (u - 1) % UNR, :], sg[:], ps[1][:, 0:F], ALU.mult).then_inc(S["a_ready"], 1)

            for i in range(2):
                for u in range(UNR):
                    estep(i, u)
            with dv.Fori(2, NIT) as i:
                for u in range(UNR):
                    estep(i, u)
            for u in range(3):
                estep(NIT, u)

            def norm_group(q):
                dv.wait_ge(S["z_rs"], q + 1)
                for t in range(4 * q, 4 * q + 4):
                    last = TS(zn[:, t, :], z[:, t, :], mvz[:, t, 0:1], rsz[:, t:t + 1], ALU.subtract, ALU.mult)
                last.then_inc(S["zn_ready"], 1)

            dv.wait_ge(S["x2_ld"], 16)
            for q in range(4):
                dv.wait_ge(y_ld[q], 32)
                for t in range(4 * q, 4 * q + 4):
                    then(STT(z[:, t, :], yk[:, 0, t, :], wtop[:, 0, t:t + 1], x2_all[:, t, :], ALU.mult, ALU.add))
                    then(STT(z[:, t, :], yk[:, 1, t, :], wtop[:, 1, t:t + 1], z[:, t, :], ALU.mult, ALU.add))
                    then(v.bn_stats(stz[:, t, :], z[:, t, :]))
                    last = v.bn_aggr(mvz[:, t, :], stz[:, t, :])
                last.then_inc(S["z_var"], 1)
                if q:
                    norm_group(q - 1)
            norm_group(3)


def layout(inputs):
    import numpy as np
    a = {k: np.asarray(v) for k, v in inputs.items()}
    x = a["x"].reshape(NTOK, D)
    dh = lambda w: w.reshape(D, H1, DH).transpose(0, 2, 1).reshape(D, D)
    wqkv = np.concatenate([dh(a["L0_attn_Wq"]), dh(a["L0_attn_Wk"]), a["L0_attn_Wv"]], axis=1)
    pairs = lambda w: w.reshape(-1, 2, NPAIR, DX).transpose(0, 2, 1, 3).reshape(-1, H2 * DX)
    two = lambda v: pairs(v).reshape(NPAIR, P).T
    biases = np.concatenate([two(a["L0_xattn_bk"]), two(a["L0_xattn_bv"]), two(a["L0_xattn_bq"]),
                             a["L0_xattn_bo"].reshape(D, 1)], axis=1)
    dn = a["L0_ffn_down_proj"]
    wdn = np.zeros((P, E, NF, D), dn.dtype)
    for k, f in enumerate(FK):
        wdn[:f, :, k, :] = dn[:, k * P:k * P + f, :].transpose(1, 0, 2)
    wgu = np.concatenate([a["L0_ffn_gate_proj"], a["L0_ffn_up_proj"]], axis=2).transpose(1, 0, 2).reshape(D, E * 2 * F)
    i, j = np.arange(P)[:, None], np.arange(P)[None, :]
    c = np.zeros((P, NCONST), np.float32)
    c[:, C_ID:C_ID + P] = i == j
    c[:, C_TRI:C_TRI + P] = i <= j
    c[:, C_BLK:C_BLK + P] = (i % H1) == (j // DH)
    c[:, C_SEG:C_SEG + P] = (j % H1) != 0
    c[:, C_REV:C_REV + P] = E - j % E
    c[:, C_IOTA:C_IOTA + P] = j
    c[:, C_ONES:C_ONES + P] = 1
    c[:, C_J128:C_J128 + NSLOT] = P * np.arange(NSLOT)
    kn = np.arange(NPK)[None, :]
    c[:, C_TOK:C_TOK + NPK] = (P * (kn % NT) + i + 1) * np.where(kn < NT, 1, -1)
    c[:, C_DUMMY:C_DUMMY + NSLOT] = TOPK * NTOK + P * np.arange(NSLOT) + i
    c[:, C_HALF:C_HALF + 16] = -0.5
    c[:, C_EPS] = EPS_LN
    cb = np.zeros((P, NCONSTB), np.float32)
    cb[:, B_ID:B_ID + P] = i == j
    cb[:, B_STRICT:B_STRICT + P] = i < j
    cb[:, B_ONE:B_ONE + P] = 1
    cb[:, B_MASK:B_MASK + HM] = np.where(np.arange(HM)[None, :] % M > i, -BIG, 0)
    return {
        "xn": x, "xT": x.T, "wqkv": wqkv, "wo1": a["L0_attn_Wo"], "bo1": a["L0_attn_bo"].reshape(D),
        "consts": c, "constb": cb.astype(mybir.dt.np(BF16)), "ctxT": a["ctx_1024"].reshape(BM, D).T,
        "wk": pairs(a["L0_xattn_Wk"]), "wv": pairs(a["L0_xattn_Wv"]),
        "wqT": pairs(a["L0_xattn_Wq"]).T.reshape(NPAIR, P, D).transpose(1, 0, 2), "biases": biases,
        "wo2": pairs(a["L0_xattn_Wo"].T).T.reshape(NPAIR, P, D).transpose(1, 0, 2), "router": a["L0_ffn_router_w"],
        "wgu": wgu, "wdn": wdn.reshape(P, E * NF * D),
    }


def kernel(**inputs):
    import numpy as np
    import concourse.bacc as bacc
    from concourse.bass_utils import run_bass_kernel_spmd

    nc = bacc.Bacc("TRN2", target_bir_lowering=False, num_devices=1)
    arrays, args = {}, []
    for name, value in layout(inputs).items():
        value = np.ascontiguousarray(value)
        arrays[f"in_{name}"] = value
        args.append(nc.dram_tensor(f"in_{name}", value.shape, mybir.dt.from_np(value.dtype), kind="ExternalInput").ap())
    out = nc.dram_tensor("out_rows", (NTOK, D), F32, kind="ExternalOutput").ap()
    decoder_layer(nc, *args, out)
    r = run_bass_kernel_spmd(nc, [arrays], core_ids=[0])
    return r.results[0]["out_rows"].reshape(B, T, D)
```

```python
from contextlib import ExitStack

import concourse.bass as bass
from concourse import mybir

F32 = mybir.dt.float32
BF16 = mybir.dt.bfloat16
F16 = mybir.dt.float16
I32 = mybir.dt.int32
ALU = mybir.AluOpType
ACT = mybir.ActivationFunctionType
AX = mybir.AxisListType

P = 128
B, T, D = 4, 512, 128
NTOK = B * T
NT = NTOK // P
TPB = T // P
H1, DH = 16, 8
H2, DX, M = 16, 64, 32
HM = H2 * M
BM = B * M
NPAIR = H2 // 2
KT4 = HM // P
E, F = 8, 352
NF = -(-F // P)
FP = NF * P
TOPK = 2
NPK = TOPK * NT
NSLOT = TOPK * NTOK // P + E - 1
UNR = 3
NIT = NSLOT // UNR
EPS_Z = 1e-6
EPS_LN = 1e-5
BIG = 1e30
assert NIT * UNR == NSLOT

C_ID = 0
C_TRI = C_ID + P
C_BLK = C_TRI + P
C_SEG = C_BLK + P
C_REV = C_SEG + P
C_IOTA = C_REV + P
C_ONES = C_IOTA + P
C_J128 = C_ONES + P
C_TOK = C_J128 + NSLOT
C_DUMMY = C_TOK + NPK
C_HALF = C_DUMMY + NSLOT
C_EPS = C_HALF + 16
C_NEG = C_EPS + 1
NCONST = C_NEG + 1
B_ID, B_STRICT, B_ONE, B_MASK = 0, P, 2 * P, 3 * P
NCONSTB = B_MASK + HM

SEMS = """ld_x ld_w1 ld_const ld_constb ld_ctx ld_wkv ld_wq ld_bias ld_wo2 ld_gu ld_dn ld_bo1
 kt_ps vt_ps kt_sb vt_sb g_ps g_sb c_ps c_hi c_r1 c_mid c_r2 c_split csT_ps csT_sb crow_zero crow_ld
 vwt_ps vwt_sb vw_ps vw_sb xb_ready
 qkv_ps er_ready v_ready feat kc_ready kq_ready den_ready z_ready kv_ready u0_ps u1_ps qu_ready intra_ready
 s_ps sblk_ready qt_ps qt_sb inter_ps comb_ready out_ready outT_ps oT_sb wo_ps y1_ready st1_ready var1_ready
 ve1_ready rs1_ready nb1_ready x1_ready x1t_ps x1t_sb sc_ps max_ready sd_ready exp_ready sum_ready rsm_ready pn_ready
 pt_ps pt_sb pv_ps y2_ready st2_ready var2_ready ve2_ready rs2_ready nb2_ready x2_ready x2_ld x2t_ps x2t_sb rt_ps
 logits_ready route e2_ready onehot_ready rank_ps rowsel_ready slot_ps idx_ready gathered xgt_ps xgt_sb
 wb_ready gate_ps up_ps silu_ready a_ready down_ps y_ready z_st dl_ready z_var z_ve z_rs zn_ready out_st""".split()


def decoder_layer(nc, xn, xT, wqkv, wo1, bo1, consts, constb, ctxT, wk, wv, wqT, biases, wo2, router,
                  wgu, wdn, out):
    x2_dram = nc.dram_tensor("x2_rows", (NTOK, D), F32, kind="Internal").ap()
    y_dram = nc.dram_tensor("expert_rows", (TOPK * NTOK + NSLOT * P, D), F32, kind="Internal").ap()

    with ExitStack() as ctx:
        def sb(name, shape, dt=F32):
            return ctx.enter_context(nc.sbuf_tensor(name, shape, dt))

        S = {n: ctx.enter_context(nc.semaphore(n)) for n in SEMS}
        xt_loaded = [ctx.enter_context(nc.semaphore(f"xt_loaded{c}")) for c in range(TPB)]
        x2_stored = [ctx.enter_context(nc.semaphore(f"x2_stored{c}")) for c in range(TPB)]
        y_ld = [ctx.enter_context(nc.semaphore(f"y_ld{g}")) for g in range(4)]
        xg_loaded = [ctx.enter_context(nc.semaphore(f"xg_loaded{c}")) for c in range(UNR)]
        y_scattered = [ctx.enter_context(nc.semaphore(f"y_scattered{c}")) for c in range(UNR)]

        c32 = sb("c32", [P, NCONST])
        cb = sb("cb", [P, NCONSTB], BF16)
        wqkv_sb = sb("wqkv_sb", [P, 3 * D])
        wo1_sb = sb("wo1_sb", [P, D])
        bo1_sb = sb("bo1_sb", [P, D])
        router_sb = sb("router_sb", [P, E])
        wgu_sb = sb("wgu_sb", [P, E * 2 * FP])
        wdn_sb = sb("wdn_sb", [P, E * NF * D])
        ident, tri = c32[:, C_ID:C_ID + P], c32[:, C_TRI:C_TRI + P]
        blockmask, segment = c32[:, C_BLK:C_BLK + P], c32[:, C_SEG:C_SEG + P]
        identb, strictb, onesb = cb[:, B_ID:B_ID + P], cb[:, B_STRICT:B_STRICT + P], cb[:, B_ONE:B_ONE + P]
        causalb = cb[:, B_MASK:B_MASK + HM]
        ctx_sb = sb("ctx_sb", [P, BM])
        early = sb("early", [P, 8 * H2 * DX])
        part = lambda k, n=1: early[:, k * H2 * DX:(k + n) * H2 * DX]
        wk_sb, wv_sb = part(0), part(1)
        wq_sb = part(2).rearrange("p (q d) -> p q d", q=NPAIR)
        wo2_sb = part(3).rearrange("p (q d) -> p q d", q=NPAIR)
        kT = part(4).rearrange("p (q m) -> p q m", q=NPAIR)
        vT = part(5).rearrange("p (q m) -> p q m", q=NPAIR)
        vwT = part(6, 2).rearrange("p (b m) -> p b m", b=B)
        yk = part(0, 4).rearrange("p (k n d) -> p k n d", k=TOPK, d=D)
        z = part(4, 2).rearrange("p (n d) -> p n d", d=D)
        zn = part(6, 2).rearrange("p (n d) -> p n d", d=D)
        bias_sb = sb("bias_sb", [P, 3 * NPAIR + 1])
        G = sb("G", [P, B, HM])
        VW = sb("VW", [P, B, KT4 * D])
        c_r = sb("c_r", [P, 2, H2])
        c_parts = sb("c_parts", [P, 3, H2], BF16)
        c_partsT = sb("c_partsT", [H2, 3, BM], BF16)
        crow = sb("crow", [P, B, HM], BF16)
        x_all = sb("x_all", [P, NT, D])
        xb_all = sb("xb_all", [P, NT, D])
        xT_sb = sb("xT_sb", [P, TPB, P])
        ex = sb("ex", [P, 2, 2 * D])
        rl = sb("rl", [P, 2, 2 * D])
        vn = sb("vn", [P, 2, D])
        qk = sb("qk", [P, 2, 2 * D])
        kcum = sb("kcum", [P, D])
        kcq = sb("kcq", [P, D + H1])
        den = sb("den", [P, H1])
        Z = sb("Z", [P, H1])
        kv = sb("kv", [P, 2, DH * D])
        qu = sb("qu", [P, DH * D])
        intra = sb("intra", [P, D])
        osum = sb("osum", [P, D])
        on_t = sb("on_t", [P, D])
        sblk = sb("sblk", [P, D])
        qT = sb("qT", [P, P])
        oT = sb("oT", [P, P])
        y1 = sb("y1", [P, 2, D])
        st = sb("st", [P, 2, 6])
        mv1 = sb("mv1", [P, 2, 2])
        ve = sb("ve", [P, 2])
        negm = sb("negm", [P, 2])
        nb1 = sb("nb1", [P, 2])
        nb2 = sb("nb2", [P, 2])
        rs1 = sb("rs1", [P, 2])
        x1 = sb("x1", [P, TPB, D])
        x1T = sb("x1T", [P, P])
        mx = sb("mx", [P, H2])
        pr = sb("pr", [P, 2, HM])
        sm = sb("sm", [P, H2])
        rsm = sb("rsm", [P, 2, H2])
        pn = sb("pn", [P, 2, HM])
        pT = sb("pT", [P, HM])
        y2 = sb("y2", [P, 2, D])
        mv2 = sb("mv2", [P, 2, 2])
        rs2 = sb("rs2", [P, 2])
        x2_ring = sb("x2_ring", [P, TPB, D])
        x2_all = sb("x2_all", [P, NT, D])
        x2T = sb("x2T", [P, P])
        logits = sb("logits", [P, NT, E])
        top = sb("top", [P, TOPK, NT])
        eq = sb("eq", [P, NT, E])
        cand = sb("cand", [P, NT, E])
        pick = sb("pick", [P, NT])
        onehot = sb("onehot", [P, TOPK, NT, E])
        l2nd = sb("l2nd", [P, NT, E])
        hotb = sb("hotb", [P, NT, E], BF16)
        dl = sb("dl", [P, NT])
        e2 = sb("e2", [P, NT])
        wtop = sb("wtop", [P, TOPK, NT])
        tot = sb("tot", [P, E, NT])
        cnt = sb("cnt", [P, E])
        cnti = sb("cnti", [P, E], I32)
        pad = sb("pad", [P, E])
        scan = sb("scan", [P, E, NT])
        base = sb("base", [P, E, NT])
        pos = sb("pos", [P, NT, E])
        posk = sb("posk", [P, TOPK, NT, E])
        slot = sb("slot", [P, NPK])
        sloti = sb("sloti", [P, NPK], I32)
        rowi = sb("rowi", [P, 2, NPK], I32)
        rowf = sb("rowf", [P, 2, NPK])
        endcmp = sb("endcmp", [P, NSLOT, E])
        texp = sb("texp", [P, NSLOT])
        texpi = sb("texpi", [P, NSLOT], I32)
        rowsel = sb("rowsel", [P, NPK, P], F16)
        tilesel = sb("tilesel", [P, NPK, NSLOT], F16)
        sv = sb("sv", [P, 4, NSLOT])
        src_row = sb("src_row", [P, NSLOT], I32)
        dst_row = sb("dst_row", [P, NSLOT], I32)
        xg = sb("xg", [P, UNR, D])
        xgT = sb("xgT", [P, UNR, P])
        wb = part(4, 4)[:, 0:UNR * 2 * FP].rearrange("p (u f) -> p u f", u=UNR)
        sg = sb("sg", [P, UNR, FP])
        aT = sb("aT", [P, UNR, FP])
        yx = sb("yx", [P, UNR, D])
        stz = sb("stz", [P, NT, 6])
        mvz = sb("mvz", [P, NT, 2])
        vez = sb("vez", [P, NT])
        rsz = sb("rsz", [P, NT])

        ps = [ctx.enter_context(nc.psum_tensor(f"bank{i}", [P, 512], F32)) for i in range(8)]
        block = ctx.enter_context(nc.Block())

        def tile_steps(eng, step, lag):
            for c in range(TPB):
                step(0, c)
            with eng.Fori(1, B) as b:
                for c in range(TPB):
                    step(b, c)
            for c in range(lag):
                step(B, c)

        def on(b, c, lag):
            return not isinstance(b, int) or 0 <= TPB * b + c - lag < NT

        def cnt_of(b, c, lag):
            return TPB * b + (c - lag + 1)

        def carries(b, c, lag):
            k = c - lag
            return 3 * (b + k // TPB) + k % TPB

        def wait(eng, sem, v):
            if not isinstance(v, int) or v > 0:
                eng.wait_ge(sem, v)

        @block.sync
        def _(sp):
            sp.dma_start(xT_sb[:, 0, :], xT[:, 0:P]).then_inc(xt_loaded[0], 16)
            sp.dma_start(wqkv_sb[:], wqkv).then_inc(S["ld_w1"], 16)
            sp.dma_start(ctx_sb[:], ctxT).then_inc(S["ld_ctx"], 16)
            sp.dma_start(wk_sb, wk).then_inc(S["ld_wkv"], 16)
            sp.dma_start(wv_sb, wv).then_inc(S["ld_wkv"], 16)
            sp.dma_start(bias_sb[:], biases).then_inc(S["ld_bias"], 16)
            sp.dma_start(c32[:], consts).then_inc(S["ld_const"], 16)
            sp.dma_start(wq_sb, wqT).then_inc(S["ld_wq"], 16)
            sp.dma_start(wo2_sb, wo2).then_inc(S["ld_wo2"], 16)
            sp.dma_start(cb[:], constb).then_inc(S["ld_constb"], 16)
            sp.dma_start(x_all[:], xn.rearrange("(n p) d -> p n d", p=P)).then_inc(S["ld_x"], 16)
            sp.dma_start(bo1_sb[:], bo1.partition_broadcast(P)).then_inc(S["ld_bo1"], 16)
            sp.dma_start(wo1_sb[:], wo1).then_inc(S["ld_w1"], 16)
            sp.dma_start(router_sb[:], router).then_inc(S["ld_w1"], 16)
            for c in range(1, TPB):
                sp.dma_start(xT_sb[:, c, :], xT[:, c * P:(c + 1) * P]).then_inc(xt_loaded[c], 16)
            sp.wait_ge(S["csT_sb"], 1)
            sp.wait_ge(S["crow_zero"], 1)
            for k in range(3):
                for b in range(B):
                    sp.dma_start(crow[k:k + 1, b, :].rearrange("o (h m) -> o h m", m=M),
                                 c_partsT[:, k, b * M:(b + 1) * M]).then_inc(S["crow_ld"], 16)
            sp.dma_start(wgu_sb[:], wgu).then_inc(S["ld_gu"], 16)
            sp.dma_start(wdn_sb[:], wdn).then_inc(S["ld_dn"], 16)

            def step(b, c):
                if not isinstance(b, int) or b < B - 1:
                    sp.wait_ge(S["qkv_ps"], cnt_of(b, c, 0))
                    sp.dma_start(xT_sb[:, c, :], xT[:, bass.ds((b + 1) * T + c * P, P)]).then_inc(xt_loaded[c], 16)
                if on(b, c, 4):
                    sp.wait_ge(S["x2_ready"], cnt_of(b, c, 4))
                    sp.dma_start(x2_dram[bass.ds((b - 1) * T + c * P, P), :],
                                 x2_ring[:, c, :]).then_inc(x2_stored[c], 16)

            for c in range(TPB):
                step(0, c)
            with sp.Fori(1, B - 1) as b:
                for c in range(TPB):
                    step(b, c)
            for b in (B - 1, B):
                for c in range(TPB):
                    step(b, c)
            for c in range(TPB):
                sp.wait_ge(x2_stored[c], 16 * (B + 1))
            sp.dma_start(x2_all[:], x2_dram.rearrange("(n p) d -> p n d", p=P)).then_inc(S["x2_ld"], 16)
            for k in range(UNR):
                sp.wait_ge(y_scattered[k], 16 * NIT)
            yv = y_dram[0:TOPK * NTOK, :].rearrange("(k n p) d -> p k n d", p=P, k=TOPK)
            for g in range(4):
                for k in range(TOPK):
                    sp.dma_start(yk[:, k, 4 * g:4 * g + 4, :], yv[:, k, 4 * g:4 * g + 4, :]).then_inc(y_ld[g], 16)
            ov = out.rearrange("(n p) d -> p n d", p=P)
            for g in range(4):
                sp.wait_ge(S["zn_ready"], g + 1)
                sp.dma_start(ov[:, 4 * g:4 * g + 4, :], zn[:, 4 * g:4 * g + 4, :]).then_inc(S["out_st"], 16)
            sp.wait_ge(S["out_st"], 64)

        @block.tensor
        def _(pe):
            mm = nc.tensor.matmul
            pe.wait_ge(S["ld_ctx"], 16)
            pe.wait_ge(S["ld_wkv"], 32)
            for w, bank, done in ((wk_sb, 0, "kt_ps"), (wv_sb, 2, "vt_ps")):
                for q in range(NPAIR):
                    last = mm(ps[bank + q // 4][:, (q % 4) * BM:(q % 4 + 1) * BM], w[:, q * P:(q + 1) * P],
                              ctx_sb[:], start=True, stop=True)
                last.then_inc(S[done], 1)
            pe.wait_ge(S["kt_sb"], 1)
            pe.wait_ge(S["ld_wq"], 16)
            for h in range(H2):
                r = slice(DX * (h // NPAIR), DX * (h // NPAIR) + DX)
                last = mm(ps[4 + h // 4][:, (h % 4) * BM:(h % 4 + 1) * BM], wq_sb[r, h % NPAIR, :], kT[r, h % NPAIR, :],
                          start=True, stop=True)
                if h % 4 == 3:
                    last.then_inc(S["g_ps"], 1)
            for h in range(H2):
                r = slice(DX * (h // NPAIR), DX * (h // NPAIR) + DX)
                last = mm(ps[h // NPAIR][:, h % NPAIR:h % NPAIR + 1], kT[r, h % NPAIR, :],
                          bias_sb[r, 2 * NPAIR + h % NPAIR:2 * NPAIR + h % NPAIR + 1],
                          start=True, stop=True)
            last.then_inc(S["c_ps"], 1)
            pe.wait_ge(S["vt_sb"], 1)
            pe.wait_ge(S["ld_wo2"], 16)
            for h in range(H2):
                r = slice(DX * (h // NPAIR), DX * (h // NPAIR) + DX)
                if h % 4 == 0:
                    pe.wait_ge(S["g_sb"], h // 4 + 1)
                last = mm(ps[4 + h // 4][:, (h % 4) * BM:(h % 4 + 1) * BM], wo2_sb[r, h % NPAIR, :], vT[r, h % NPAIR, :],
                          start=True, stop=True)
                if h % 4 == 3:
                    last.then_inc(S["vwt_ps"], 1)
            pe.wait_ge(S["c_split"], 1)
            pe.wait_ge(S["ld_constb"], 16)
            for k in range(3):
                last = nc.tensor.transpose(ps[2].bitcast(BF16)[0:H2, k * BM:(k + 1) * BM], c_parts[:, k, :], identb)
            last.then_inc(S["csT_ps"], 1)
            pe.wait_ge(S["vwt_sb"], 4)
            pe.wait_ge(S["ld_const"], 16)
            for b in range(B):
                for k in range(KT4):
                    last = nc.tensor.transpose(ps[4 + b][:, k * D:(k + 1) * D], vwT[:, b, k * P:(k + 1) * P], ident)
                last.then_inc(S["vw_ps"], 1)

            def step(b, c):
                n = lambda lag: cnt_of(b, c, lag)
                carried = c > 0
                batch = lambda lag: b + (c - lag) // TPB
                row = lambda t, bb: t[:, bb, :] if isinstance(bb, int) else t[:, bass.ds(bb, 1), :]
                if on(b, c, 0):
                    pe.wait_ge(xt_loaded[c], 16 * (b + 1))
                    mm(ps[0][:, 0:3 * D], xT_sb[:, c, :], wqkv_sb[:], start=True, stop=True).then_inc(S["qkv_ps"], 1)
                if on(b, c, 2):
                    pe.wait_ge(S["x1_ready"], n(2))
                    nc.tensor.transpose(ps[4][:, 2 * P:3 * P], x1[:, (c - 2) % TPB, :], ident).then_inc(S["x1t_ps"], 1)
                if on(b, c, 3):
                    pe.wait_ge(S["pn_ready"], n(3))
                    wait(pe, S["y2_ready"], n(4))
                    s2 = (c - 3) % 2
                    for k in range(KT4):
                        last = nc.tensor.transpose(ps[6][:, k * P:(k + 1) * P], pn[:, s2, k * P:(k + 1) * P], ident)
                    last.then_inc(S["pt_ps"], 1)
                if on(b, c, 2):
                    pe.wait_ge(S["x1t_sb"], n(2))
                    bb = batch(2)
                    first = (c - 2) % TPB == 0
                    mm(ps[5][:], x1T[:], row(G, bb), start=True, stop=False)
                    last = mm(ps[5][:], onesb, row(crow, bb), start=False, stop=not first)
                    if first:
                        last = mm(ps[5][:], identb, causalb, start=False, stop=True)
                    last.then_inc(S["sc_ps"], 1)
                if on(b, c, 1):
                    pe.wait_ge(S["out_ready"], n(1))
                    nc.tensor.transpose(ps[7][:, 0:P], on_t[:], ident).then_inc(S["outT_ps"], 1)
                if on(b, c, 3):
                    pe.wait_ge(S["pt_sb"], n(3))
                    bb = batch(3)
                    for k in range(KT4):
                        last = mm(ps[6][:, 0:D], pT[:, k * P:(k + 1) * P], VW[:, bb, k * D:(k + 1) * D]
                                  if isinstance(bb, int) else VW[:, bass.ds(bb, 1), k * D:(k + 1) * D],
                                  start=k == 0, stop=k == KT4 - 1)
                    last.then_inc(S["pv_ps"], 1)
                if on(b, c, 4):
                    pe.wait_ge(S["x2_ready"], n(4))
                    if not on(b, c, 2):
                        wait(pe, S["logits_ready"], n(5))
                    nc.tensor.transpose(ps[4][:, 0:P], x2_ring[:, c, :], ident).then_inc(S["x2t_ps"], 1)
                if on(b, c, 1):
                    pe.wait_ge(S["oT_sb"], n(1))
                    mm(ps[7][:, P:P + D], oT[:], wo1_sb[:], start=True, stop=True).then_inc(S["wo_ps"], 1)
                if on(b, c, 0) and carried:
                    pe.wait_ge(S["feat"], n(0))
                    pe.wait_ge(S["v_ready"], n(0))
                    nc.tensor.transpose(ps[0][:, 0:P], qk[:, c % 2, 0:D], ident).then_inc(S["qt_ps"], 1)
                if on(b, c, 4):
                    pe.wait_ge(S["x2t_sb"], n(4))
                    mm(ps[4][:, P:P + E], x2T[:], router_sb[:], start=True, stop=True).then_inc(S["rt_ps"], 1)
                def running_sum(k):
                    mm(ps[1 + k][:], tri, kv[:, c % 2, k * 512:(k + 1) * 512], start=True,
                       stop=True).then_inc(S[f"u{k}_ps"], 1)
                if on(b, c, 0):
                    pe.wait_ge(S["kv_ready"], n(0))
                    running_sum(0)
                if on(b, c, 0):
                    running_sum(1)
                if on(b, c, 0) and carried:
                    pe.wait_ge(S["qt_sb"], carries(b, c, 0))
                    wait(pe, S["y1_ready"], n(1))
                    mm(ps[7][:, 2 * P:2 * P + D], qT[:], sblk[:], start=True, stop=True).then_inc(S["inter_ps"], 1)
                if on(b, c, 0) and c < TPB - 1:
                    if not carried:
                        wait(pe, S["sblk_ready"], carries(b, c, 0))
                    mm(ps[3][:, 0:D], qk[:, c % 2, D:2 * D], vn[:, c % 2, :], start=c == 0, stop=True,
                       skip_group_check=True).then_inc(S["s_ps"], 1)

            pe.wait_ge(S["crow_ld"], 3 * B * 16)
            pe.wait_ge(S["vw_sb"], 4)
            pe.wait_ge(S["ld_w1"], 48)
            tile_steps(pe, step, 4)

            pe.wait_ge(S["onehot_ready"], 1)
            hb = hotb[:].rearrange("p n e -> p (n e)")
            mm(ps[0][:, 0:P], strictb, hb, start=True, stop=True)
            mm(ps[0][:, P:2 * P], onesb, hb, start=True, stop=True).then_inc(S["rank_ps"], 1)
            for i in range(NPK):
                if i % 8 == 0:
                    pe.wait_ge(S["rowsel_ready"], i // 8 + 1)
                last = mm(ps[1][:, 0:NSLOT], rowsel[:, i, :], tilesel[:, i, :], start=i == 0, stop=i == NPK - 1)
            last.then_inc(S["slot_ps"], 1)
            pe.wait_ge(S["idx_ready"], 1)
            pe.wait_ge(S["ld_gu"], 16)
            pe.wait_ge(S["ld_dn"], 16)

            def estep(i, u):
                has = lambda lag: not isinstance(i, int) or 0 <= UNR * i + u - lag < NSLOT
                n = lambda lag: UNR * i + (u - lag + 1)
                sl = lambda lag: (u - lag) % UNR
                if has(1):
                    pe.wait_ge(S["wb_ready"], n(1))
                    pe.wait_ge(S["xgt_sb"], n(1))
                    wait(pe, S["silu_ready"], n(2))
                    for k in range(NF):
                        last = mm(ps[0][:, k * P:(k + 1) * P], wb[:, sl(1), k * P:(k + 1) * P], xgT[:, sl(1), :],
                                  start=True, stop=True)
                    last.then_inc(S["gate_ps"], 1)
                if has(0):
                    pe.wait_ge(xg_loaded[u], 16 * (i + 1))
                    wait(pe, S["xgt_sb"], n(1))
                    nc.tensor.transpose(ps[4][:, 0:P], xg[:, u, :], ident).then_inc(S["xgt_ps"], 1)
                if has(1):
                    wait(pe, S["a_ready"], n(2))
                    for k in range(NF):
                        last = mm(ps[1][:, k * P:(k + 1) * P], wb[:, sl(1), FP + k * P:FP + (k + 1) * P],
                                  xgT[:, sl(1), :], start=True, stop=True)
                    last.then_inc(S["up_ps"], 1)
                if has(2):
                    ed = pe.value_load(texpi[0:1, bass.ds(UNR * i + (u - 2), 1)], min_val=0, max_val=E - 1)
                    pe.wait_ge(S["a_ready"], n(2))
                    wait(pe, S["y_ready"], n(3))
                    for k in range(NF):
                        last = mm(ps[3][:, 0:D], aT[:, sl(2), k * P:(k + 1) * P],
                                  wdn_sb[:, bass.ds(ed * (NF * D) + k * D, D)], start=k == 0, stop=k == NF - 1)
                    last.then_inc(S["down_ps"], 1)

            for i in range(2):
                for u in range(UNR):
                    estep(i, u)
            with pe.Fori(2, NIT) as i:
                for u in range(UNR):
                    estep(i, u)
            for u in range(3):
                estep(NIT, u)

        @block.scalar
        def _(ac):
            act_f = nc.scalar.activation
            for g in range(4):
                ac.wait_ge(S["g_ps"], g + 1)
                act_f(G[:, :, g * P:(g + 1) * P].rearrange("p b (h m) -> p h b m", m=M),
                      ps[4 + g][:].rearrange("p (h b m) -> p h b m", b=B, m=M), ACT.Copy).then_inc(S["g_sb"], 1)
            ac.wait_ge(S["csT_ps"], 1)
            act_f(c_partsT[:].rearrange("p k m -> p (k m)"), ps[2].bitcast(BF16)[0:H2, 0:3 * BM], ACT.Copy).then_inc(S["csT_sb"], 1)
            for b in range(B):
                ac.wait_ge(S["vw_ps"], b + 1)
                act_f(VW[:, b, :], ps[4 + b][:], ACT.Copy).then_inc(S["vw_sb"], 1)

            def step(b, c):
                n = lambda lag: cnt_of(b, c, lag)
                if on(b, c, 0):
                    s2 = c % 2
                    ac.wait_ge(S["qkv_ps"], n(0))
                    act_f(ex[:, s2, :], ps[0][:, 0:2 * D], ACT.Exp)
                    act_f(rl[:, s2, :], ps[0][:, 0:2 * D], ACT.Relu).then_inc(S["er_ready"], 1)
                if on(b, c, 2):
                    ac.wait_ge(S["x1t_ps"], n(2))
                    act_f(x1T[:], ps[4][:, 2 * P:3 * P], ACT.Copy).then_inc(S["x1t_sb"], 1)
                if on(b, c, 0):
                    act_f(vn[:, c % 2, :], ps[0][:, 2 * D:3 * D], ACT.Copy).then_inc(S["v_ready"], 1)
                if on(b, c, 3):
                    ac.wait_ge(S["pt_ps"], n(3))
                    act_f(pT[:], ps[6][:], ACT.Copy).then_inc(S["pt_sb"], 1)
                if on(b, c, 4):
                    ac.wait_ge(S["nb2_ready"], n(4))
                    ac.wait_ge(x2_stored[c], 16 * b)
                    act_f(x2_ring[:, c, :], y2[:, c % 2, :], ACT.Identity, bias=nb2[:, c % 2:c % 2 + 1],
                          scale=rs2[:, c % 2:c % 2 + 1]).then_inc(S["x2_ready"], 1)
                if on(b, c, 1):
                    ac.wait_ge(S["outT_ps"], n(1))
                    act_f(oT[:], ps[7][:, 0:P], ACT.Copy).then_inc(S["oT_sb"], 1)
                if on(b, c, 4):
                    ac.wait_ge(S["x2t_ps"], n(4))
                    act_f(x2T[:], ps[4][:, 0:P], ACT.Copy).then_inc(S["x2t_sb"], 1)
                if on(b, c, 0) and c > 0:
                    ac.wait_ge(S["qt_ps"], carries(b, c, 0))
                    act_f(qT[:], ps[0][:, 0:P], ACT.Copy).then_inc(S["qt_sb"], 1)
                if on(b, c, 2):
                    ac.wait_ge(S["sd_ready"], n(2))
                    act_f(pr[:, c % 2, :], pr[:, c % 2, :], ACT.Exp, scale=float(DX) ** -0.5).then_inc(S["exp_ready"], 1)
                if on(b, c, 1):
                    s2 = (c - 1) % 2
                    ac.wait_ge(S["nb1_ready"], n(1))
                    act_f(x1[:, (c - 1) % TPB, :], y1[:, s2, :], ACT.Identity, bias=nb1[:, s2:s2 + 1],
                          scale=rs1[:, s2:s2 + 1]).then_inc(S["x1_ready"], 1)

            tile_steps(ac, step, 4)
            ac.wait_ge(S["dl_ready"], 1)
            act_f(e2[:], dl[:], ACT.Exp).then_inc(S["e2_ready"], 1)

            ac.wait_ge(S["idx_ready"], 1)
            ac.wait_ge(S["ld_gu"], 16)

            def estep(i, u):
                has = lambda lag: not isinstance(i, int) or 0 <= UNR * i + u - lag < NSLOT
                n = lambda lag: UNR * i + (u - lag + 1)
                if has(0):
                    e = ac.value_load(texpi[0:1, bass.ds(UNR * i + u, 1)], min_val=0, max_val=E - 1)
                    act_f(wb[:, u, :], wgu_sb[:, bass.ds(e * (2 * FP), 2 * FP)], ACT.Copy).then_inc(S["wb_ready"], 1)
                if has(1):
                    ac.wait_ge(S["gate_ps"], n(1))
                    wait(ac, S["a_ready"], n(4))
                    act_f(sg[:, (u - 1) % UNR, :], ps[0][:, 0:FP], ACT.Silu).then_inc(S["silu_ready"], 1)
                if has(0):
                    ac.wait_ge(S["xgt_ps"], n(0))
                    wait(ac, S["up_ps"], UNR * i + u - UNR + 1)
                    act_f(xgT[:, u, :], ps[4][:, 0:P], ACT.Copy).then_inc(S["xgt_sb"], 1)

            for i in range(2):
                for u in range(UNR):
                    estep(i, u)
            with ac.Fori(2, NIT) as i:
                for u in range(UNR):
                    estep(i, u)
            for u in range(3):
                estep(NIT, u)

        @block.gpsimd
        def _(pool):
            g = nc.gpsimd
            g.memset(crow[:], 0.0).then_inc(S["crow_zero"], 1)
            pool.wait_ge(S["ld_x"], 16)
            pool.wait_ge(S["ld_bo1"], 16)
            g.tensor_tensor(xb_all[:], x_all[:], bo1_sb[:].unsqueeze(1).broadcast_to([P, NT, D]),
                            ALU.add).then_inc(S["xb_ready"], 1)
            pool.wait_ge(S["ld_const"], 16)
            half = c32[:, C_HALF:C_HALF + 1]
            eps = c32[:, C_EPS:C_EPS + 1]
            neg1 = c32[:, C_NEG:C_NEG + 1]

            def normaliser(k, mv, rs, nb, s2, n):
                pool.wait_ge(S[f"var{k}_ready"], n)
                g.tensor_tensor(negm[:, k - 1:k], mv[:, s2, 0:1], neg1, ALU.mult)
                g.tensor_tensor(ve[:, k - 1:k], mv[:, s2, 1:2], eps, ALU.add).then_inc(S[f"ve{k}_ready"], 1)
                pool.wait_ge(S[f"ve{k}_ready"], n)
                g.tensor_tensor(rs[:, s2:s2 + 1], ve[:, k - 1:k], half, ALU.pow).then_inc(S[f"rs{k}_ready"], 1)
                pool.wait_ge(S[f"rs{k}_ready"], n)
                g.tensor_tensor(nb[:, s2:s2 + 1], rs[:, s2:s2 + 1], negm[:, k - 1:k],
                                ALU.mult).then_inc(S[f"nb{k}_ready"], 1)

            def step(b, c):
                n = lambda lag: cnt_of(b, c, lag)
                if on(b, c, 0):
                    s2 = c % 2
                    pool.wait_ge(S["feat"], n(0))
                    pool.wait_ge(S["v_ready"], n(0))
                    g.tensor_tensor(kv[:, s2, :].rearrange("p (d h e) -> p d h e", d=DH, e=DH),
                                    qk[:, s2, D:2 * D].rearrange("p (d h) -> p d h", d=DH).unsqueeze(3)
                                    .broadcast_to([P, DH, H1, DH]),
                                    vn[:, s2, :].rearrange("p (h e) -> p h e", e=DH).unsqueeze(1)
                                    .broadcast_to([P, DH, H1, DH]), ALU.mult).then_inc(S["kv_ready"], 1)
                if on(b, c, 1):
                    normaliser(1, mv1, rs1, nb1, (c - 1) % 2, n(1))
                if on(b, c, 2):
                    s2 = (c - 2) % 2
                    pool.wait_ge(S["rsm_ready"], n(2))
                    g.tensor_tensor(pn[:, s2, :].rearrange("p (h m) -> p h m", m=M),
                                    pr[:, s2, :].rearrange("p (h m) -> p h m", m=M),
                                    rsm[:, s2, :].unsqueeze(2).broadcast_to([P, H2, M]), ALU.mult).then_inc(S["pn_ready"], 1)
                if on(b, c, 3):
                    normaliser(2, mv2, rs2, nb2, (c - 3) % 2, n(3))

            tile_steps(pool, step, 4)

            pool.wait_ge(S["idx_ready"], 1)
            for c in range(TPB):
                pool.wait_ge(x2_stored[c], 16 * (B + 1))
            for j in range(NSLOT + 6):
                if 0 <= j - 6:
                    t = j - 6
                    pool.wait_ge(S["y_ready"], t + 1)
                    g.indirect_dma_start(y_dram, bass.IndirectOffsetOnAxis(ap=dst_row[:, t:t + 1], axis=0),
                                         yx[:, t % UNR, :], None).then_inc(y_scattered[t % UNR], 16)
                if j < NSLOT:
                    if j >= UNR:
                        pool.wait_ge(S["xgt_ps"], j - UNR + 1)
                    g.indirect_dma_start(xg[:, j % UNR, :], None, x2_dram,
                                         bass.IndirectOffsetOnAxis(ap=src_row[:, j:j + 1], axis=0)
                                         ).then_inc(xg_loaded[j % UNR], 16)
            for q in range(4):
                pool.wait_ge(S["z_var"], q + 1)
                sl = slice(4 * q, 4 * q + 4)
                g.tensor_tensor(vez[:, sl], mvz[:, sl, 1], eps.broadcast_to([P, 4]), ALU.add).then_inc(S["z_ve"], 1)
                pool.wait_ge(S["z_ve"], q + 1)
                g.tensor_tensor(rsz[:, sl], vez[:, sl], c32[:, C_HALF:C_HALF + 4], ALU.pow).then_inc(S["z_rs"], 1)

        @block.vector
        def _(dv):
            v = nc.vector
            TT, TS, STT = v.tensor_tensor, v.tensor_scalar, v.scalar_tensor_tensor
            dv.wait_ge(S["ld_bias"], 16)
            for t, bank, col, src, done in ((kT, 0, 0, "kt_ps", "kt_sb"), (vT, 2, NPAIR, "vt_ps", "vt_sb")):
                dv.wait_ge(S[src], 1)
                for k in range(2):
                    last = TT(t[:, 4 * k:4 * k + 4, :], ps[bank + k][:].rearrange("p (q m) -> p q m", q=4),
                              bias_sb[:, col + 4 * k:col + 4 * k + 4].unsqueeze(2).broadcast_to([P, 4, BM]), ALU.add)
                last.then_inc(S[done], 1)
            dv.wait_ge(S["c_ps"], 1)
            for g in range(2):
                hs = slice(g * NPAIR, g * NPAIR + NPAIR)
                last = v.tensor_copy(c_parts[:, 0, hs], ps[g][:, 0:NPAIR])
            last.then_inc(S["c_hi"], 1)
            dv.wait_ge(S["c_hi"], 1)
            for g in range(2):
                hs = slice(g * NPAIR, g * NPAIR + NPAIR)
                last = TT(c_r[:, 0, hs], ps[g][:, 0:NPAIR], c_parts[:, 0, hs], ALU.subtract)
            last.then_inc(S["c_r1"], 1)
            dv.wait_ge(S["c_r1"], 1)
            v.tensor_copy(c_parts[:, 1, :], c_r[:, 0, :]).then_inc(S["c_mid"], 1)
            dv.wait_ge(S["c_mid"], 1)
            TT(c_r[:, 1, :], c_r[:, 0, :], c_parts[:, 1, :], ALU.subtract).then_inc(S["c_r2"], 1)
            dv.wait_ge(S["c_r2"], 1)
            v.tensor_copy(c_parts[:, 2, :], c_r[:, 1, :]).then_inc(S["c_split"], 1)
            for k in range(4):
                dv.wait_ge(S["vwt_ps"], k + 1)
                src = ps[4 + k][:].rearrange("p (h b m) -> p h b m", b=B, m=M)
                dst = vwT[:, :, k * P:(k + 1) * P].rearrange("p b (h m) -> p h b m", m=M)
                if k == 0:
                    TS(dst[:, 0], src[:, 0], bias_sb[:, 3 * NPAIR:3 * NPAIR + 1], None, ALU.add)
                    v.tensor_copy(dst[:, 1:4], src[:, 1:4]).then_inc(S["vwt_sb"], 1)
                else:
                    v.tensor_copy(dst, src).then_inc(S["vwt_sb"], 1)
            dv.wait_ge(S["xb_ready"], 1)
            dv.wait_ge(S["ld_const"], 16)
            for c in range(TPB):
                dv.sem_inc(x2_stored[c], 16)

            v.memset(kcq[:, D:D + H1], EPS_Z)

            def step(b, c):
                n = lambda lag: cnt_of(b, c, lag)
                tile = lambda t, lag: t[:, bass.ds(TPB * b + (c - lag), 1), :]
                if on(b, c, 1):
                    dv.wait_ge(S["qu_ready"], n(1))
                    v.tensor_reduce(intra[:], qu[:].rearrange("p (d f) -> p f d", d=DH), AX.X, ALU.add).then_inc(S["intra_ready"], 1)
                if on(b, c, 0):
                    s2 = c % 2
                    dv.wait_ge(S["er_ready"], n(0))
                    STT(qk[:, s2, :], ex[:, s2, :], 1.0, rl[:, s2, :], ALU.min, ALU.add).then_inc(S["feat"], 1)
                if on(b, c, 1) and c > 0:
                    dv.wait_ge(S["s_ps"], carries(b, c, 0))
                    TT(sblk[:], ps[3][:, 0:D], blockmask, ALU.mult).then_inc(S["sblk_ready"], 1)
                if on(b, c, 1) and (c - 1) % TPB:
                    dv.wait_ge(S["intra_ready"], n(1))
                    dv.wait_ge(S["inter_ps"], carries(b, c, 1))
                    TT(osum[:], ps[7][:, 2 * P:2 * P + D], intra[:], ALU.add).then_inc(S["comb_ready"], 1)
                if on(b, c, 0):
                    dv.wait_ge(S["feat"], n(0))
                    v.tensor_tensor_scan(kcum[:], segment, qk[:, c % 2, D:2 * D], 0.0,
                                         ALU.mult, ALU.add).then_inc(S["kc_ready"], 1)
                if on(b, c, 1):
                    o3 = on_t[:].rearrange("p (h e) -> p h e", e=DH)
                    zb = Z[:].unsqueeze(2).broadcast_to([P, H1, DH])
                    dv.wait_ge(S["z_ready"], n(1))
                    if (c - 1) % TPB:
                        dv.wait_ge(S["comb_ready"], carries(b, c, 1))
                        TT(o3, osum[:].rearrange("p (h e) -> p h e", e=DH), zb, ALU.mult).then_inc(S["out_ready"], 1)
                    else:
                        dv.wait_ge(S["intra_ready"], n(1))
                        TT(o3, intra[:].rearrange("p (h e) -> p h e", e=DH), zb, ALU.mult).then_inc(S["out_ready"], 1)
                if on(b, c, 0):
                    dv.wait_ge(S["kc_ready"], n(0))
                    TT(kcq[:, 0:D], kcum[:], qk[:, c % 2, 0:D], ALU.mult).then_inc(S["kq_ready"], 1)
                if on(b, c, 2):
                    s3 = ps[5][:].rearrange("p (h m) -> p h m", m=M)
                    dv.wait_ge(S["sc_ps"], n(2))
                    v.tensor_reduce(mx[:], s3, AX.X, ALU.max).then_inc(S["max_ready"], 1)
                if on(b, c, 0):
                    dv.wait_ge(S["kq_ready"], n(0))
                    v.tensor_reduce(den[:], kcq[:].rearrange("p (d h) -> p h d", d=DH + 1), AX.X,
                                    ALU.add).then_inc(S["den_ready"], 1)
                if on(b, c, 2):
                    s2 = (c - 2) % 2
                    dv.wait_ge(S["max_ready"], n(2))
                    TT(pr[:, s2, :].rearrange("p (h m) -> p h m", m=M), s3,
                       mx[:].unsqueeze(2).broadcast_to([P, H2, M]), ALU.subtract).then_inc(S["sd_ready"], 1)
                if on(b, c, 0):
                    dv.wait_ge(S["den_ready"], n(0))
                    v.reciprocal(Z[:], den[:]).then_inc(S["z_ready"], 1)
                if on(b, c, 1):
                    dv.wait_ge(S["wo_ps"], n(1))
                    TT(y1[:, (c - 1) % 2, :].unsqueeze(1), ps[7][:, P:P + D].unsqueeze(1), tile(xb_all, 1),
                       ALU.add).then_inc(S["y1_ready"], 1)
                if on(b, c, 3):
                    dv.wait_ge(S["pv_ps"], n(3))
                    TT(y2[:, (c - 3) % 2, :], ps[6][:, 0:D], x1[:, (c - 3) % TPB, :], ALU.add).then_inc(S["y2_ready"], 1)
                if on(b, c, 1):
                    dv.wait_ge(S["y1_ready"], n(1))
                    v.bn_stats(st[:, 0, :], y1[:, (c - 1) % 2, :]).then_inc(S["st1_ready"], 1)
                if on(b, c, 3):
                    dv.wait_ge(S["y2_ready"], n(3))
                    v.bn_stats(st[:, 1, :], y2[:, (c - 3) % 2, :]).then_inc(S["st2_ready"], 1)
                if on(b, c, 1):
                    dv.wait_ge(S["st1_ready"], n(1))
                if on(b, c, 4):
                    dv.wait_ge(S["rt_ps"], n(4))
                    v.tensor_copy(tile(logits, 4), ps[4][:, P:P + E].unsqueeze(1)).then_inc(S["logits_ready"], 1)
                if on(b, c, 1):
                    v.bn_aggr(mv1[:, (c - 1) % 2, :], st[:, 0, :]).then_inc(S["var1_ready"], 1)
                if on(b, c, 3):
                    dv.wait_ge(S["st2_ready"], n(3))
                if on(b, c, 2):
                    s2 = (c - 2) % 2
                    dv.wait_ge(S["exp_ready"], n(2))
                    v.tensor_reduce(sm[:], pr[:, s2, :].rearrange("p (h m) -> p h m", m=M), AX.X, ALU.add).then_inc(S["sum_ready"], 1)
                if on(b, c, 3):
                    v.bn_aggr(mv2[:, (c - 3) % 2, :], st[:, 1, :]).then_inc(S["var2_ready"], 1)
                if on(b, c, 2):
                    dv.wait_ge(S["sum_ready"], n(2))
                    v.reciprocal(rsm[:, (c - 2) % 2, :], sm[:]).then_inc(S["rsm_ready"], 1)
                def q_times_sum(k):
                    dv.wait_ge(S[f"u{k}_ps"], n(0))
                    return TT(qu[:, 512 * k:512 * k + 512].rearrange("p (a e) -> p a e", e=DH),
                              ps[1 + k][:].rearrange("p (a e) -> p a e", e=DH),
                              qk[:, c % 2, 64 * k:64 * k + 64].unsqueeze(2).broadcast_to([P, 64, DH]), ALU.mult)
                if on(b, c, 0):
                    q_times_sum(0)
                if on(b, c, 0):
                    q_times_sum(1).then_inc(S["qu_ready"], 1)

            tile_steps(dv, step, 4)

            count = [0]

            def then(ins):
                count[0] += 1
                ins.then_inc(S["route"], 1)
                dv.wait_ge(S["route"], count[0])

            dv.wait_ge(S["logits_ready"], NT)
            rev = c32[:, C_REV:C_REV + P].rearrange("p (n e) -> p n e", e=E)
            lane = lambda t: t.unsqueeze(2).broadcast_to([P, NT, E])
            for k in range(TOPK):
                src = logits if k == 0 else l2nd
                then(v.tensor_reduce(top[:, k, :], src[:], AX.X, ALU.max))
                then(TT(eq[:], src[:], lane(top[:, k, :]), ALU.is_equal))
                then(TT(cand[:], eq[:], rev, ALU.mult))
                then(v.tensor_reduce(pick[:], cand[:], AX.X, ALU.max))
                then(TT(onehot[:, k], rev, lane(pick[:]), ALU.is_equal))
                if k == 0:
                    then(STT(l2nd[:], onehot[:, 0], -3e38, logits[:], ALU.mult, ALU.add))
            TT(hotb[:], onehot[:, 0], onehot[:, 1], ALU.add).then_inc(S["onehot_ready"], 1)
            TT(dl[:], top[:, 1, :], top[:, 0, :], ALU.subtract).then_inc(S["dl_ready"], 1)
            dv.wait_ge(S["e2_ready"], 1)
            then(TS(wtop[:, 1, :], e2[:], 1.0, None, ALU.add))
            then(v.reciprocal(wtop[:, 0, :], wtop[:, 1, :]))
            then(TT(wtop[:, 1, :], wtop[:, 0, :], e2[:], ALU.mult))
            dv.wait_ge(S["rank_ps"], 1)
            then(v.tensor_copy(tot[:], ps[0][:, P:2 * P].rearrange("p (n e) -> p e n", e=E)))
            then(v.tensor_reduce(cnt[:], tot[:], AX.X, ALU.add))
            then(TS(cnti[:], cnt[:], float(P - 1), None, ALU.add))
            then(TS(cnti[:], cnti[:], ~(P - 1), None, ALU.bitwise_and))
            then(TT(pad[:], cnti[:], cnt[:], ALU.subtract))
            then(TT(tot[:, :, NT - 1], tot[:, :, NT - 1], pad[:], ALU.add))
            ones_row = c32[:, C_ONES:C_ONES + P]
            flat = lambda t: t[:].rearrange("p e n -> p (e n)")
            then(v.tensor_tensor_scan(flat(scan), ones_row, flat(tot), 0.0, ALU.mult, ALU.add))
            then(TT(base[:], scan[:], tot[:], ALU.subtract))
            then(TT(pos[:], ps[0][:, 0:P].rearrange("p (n e) -> p n e", e=E), base[:].rearrange("p e n -> p n e"), ALU.add))
            for k in range(TOPK):
                then(TT(posk[:, k], onehot[:, k], pos[:], ALU.mult))
            then(v.tensor_reduce(slot[:], posk[:].rearrange("p k n e -> p (k n) e"), AX.X, ALU.add))
            then(v.tensor_copy(sloti[:], slot[:]))
            then(TS(rowi[:, 0, :], sloti[:], P - 1, None, ALU.bitwise_and))
            then(TS(rowi[:, 1, :], sloti[:], P.bit_length() - 1, None, ALU.logical_shift_right))
            then(v.tensor_copy(rowf[:], rowi[:]))
            iota = c32[:, C_IOTA:C_IOTA + P]
            token = c32[:, C_TOK:C_TOK + NPK]
            for i in range(NPK):
                TS(rowsel[:, i, :], iota, rowf[:, 0, i:i + 1], None, ALU.is_equal)
                last = TS(tilesel[:, i, :], iota[:, 0:NSLOT], rowf[:, 1, i:i + 1], token[:, i:i + 1], ALU.is_equal, ALU.mult)
                if i % 8 == 7:
                    last.then_inc(S["rowsel_ready"], 1)
            then(TT(endcmp[:], c32[:, C_J128:C_J128 + NSLOT].unsqueeze(2).broadcast_to([P, NSLOT, E]),
                    scan[:, :, NT - 1].unsqueeze(1).broadcast_to([P, NSLOT, E]), ALU.is_ge))
            then(v.tensor_reduce(texp[:], endcmp[:], AX.X, ALU.add))
            then(TS(texpi[:], texp[:], float(E - 1), None, ALU.min))
            dv.wait_ge(S["slot_ps"], 1)
            then(v.tensor_copy(sv[:, 0, :], ps[1][:, 0:NSLOT]))
            then(STT(sv[:, 2, :], sv[:, 0, :], -1.0, sv[:, 0, :], ALU.mult, ALU.max))
            then(TS(sv[:, 1, :], sv[:, 2, :], 1.0, -1.0, ALU.max, ALU.add))
            then(v.tensor_copy(src_row[:], sv[:, 1, :]))
            then(TS(sv[:, 2, :], sv[:, 0, :], 0.0, float(NTOK), ALU.is_lt, ALU.mult))
            then(TT(sv[:, 1, :], sv[:, 1, :], sv[:, 2, :], ALU.add))
            then(STT(sv[:, 3, :], sv[:, 0, :], 0.0, c32[:, C_DUMMY:C_DUMMY + NSLOT], ALU.is_equal, ALU.mult))
            TT(dst_row[:], sv[:, 1, :], sv[:, 3, :], ALU.add).then_inc(S["idx_ready"], 1)

            def estep(i, u):
                has = lambda lag: not isinstance(i, int) or 0 <= UNR * i + u - lag < NSLOT
                n = lambda lag: UNR * i + (u - lag + 1)
                sl = (u - 1) % UNR
                if has(3):
                    dv.wait_ge(S["down_ps"], n(3))
                    wait(dv, y_scattered[u], 16 * (i - 1))
                    v.tensor_copy(yx[:, u, :], ps[3][:, 0:D]).then_inc(S["y_ready"], 1)
                if has(1):
                    dv.wait_ge(S["silu_ready"], n(1))
                    dv.wait_ge(S["up_ps"], n(1))
                    wait(dv, S["down_ps"], UNR * i + (u - 1) - UNR + 1)
                    TT(aT[:, sl, :], sg[:, sl, :], ps[1][:, 0:FP], ALU.mult).then_inc(S["a_ready"], 1)

            for i in range(2):
                for u in range(UNR):
                    estep(i, u)
            with dv.Fori(2, NIT) as i:
                for u in range(UNR):
                    estep(i, u)
            for u in range(3):
                estep(NIT, u)

            def norm_group(q):
                dv.wait_ge(S["z_rs"], q + 1)
                for t in range(4 * q, 4 * q + 4):
                    last = TS(zn[:, t, :], z[:, t, :], mvz[:, t, 0:1], rsz[:, t:t + 1], ALU.subtract, ALU.mult)
                last.then_inc(S["zn_ready"], 1)

            dv.wait_ge(S["x2_ld"], 16)
            for q in range(4):
                dv.wait_ge(y_ld[q], 32)
                for t in range(4 * q, 4 * q + 4):
                    then(STT(z[:, t, :], yk[:, 0, t, :], wtop[:, 0, t:t + 1], x2_all[:, t, :], ALU.mult, ALU.add))
                    then(STT(z[:, t, :], yk[:, 1, t, :], wtop[:, 1, t:t + 1], z[:, t, :], ALU.mult, ALU.add))
                    then(v.bn_stats(stz[:, t, :], z[:, t, :]))
                    last = v.bn_aggr(mvz[:, t, :], stz[:, t, :])
                last.then_inc(S["z_var"], 1)
                if q:
                    norm_group(q - 1)
            norm_group(3)


def layout(inputs):
    import numpy as np
    a = {k: np.asarray(v) for k, v in inputs.items()}
    x = a["x"].reshape(NTOK, D)
    dh = lambda w: w.reshape(D, H1, DH).transpose(0, 2, 1).reshape(D, D)
    wqkv = np.concatenate([dh(a["L0_attn_Wq"]), dh(a["L0_attn_Wk"]), a["L0_attn_Wv"]], axis=1)
    pairs = lambda w: w.reshape(-1, 2, NPAIR, DX).transpose(0, 2, 1, 3).reshape(-1, H2 * DX)
    two = lambda v: pairs(v).reshape(NPAIR, P).T
    biases = np.concatenate([two(a["L0_xattn_bk"]), two(a["L0_xattn_bv"]), two(a["L0_xattn_bq"]),
                             a["L0_xattn_bo"].reshape(D, 1)], axis=1)
    dn = a["L0_ffn_down_proj"]
    wdn = np.zeros((E, FP, D), dn.dtype)
    wdn[:, :F] = dn
    wdn = wdn.reshape(E, NF, P, D).transpose(2, 0, 1, 3)
    wgu = np.zeros((D, E, 2, FP), dn.dtype)
    wgu[:, :, 0, :F] = a["L0_ffn_gate_proj"].transpose(1, 0, 2)
    wgu[:, :, 1, :F] = a["L0_ffn_up_proj"].transpose(1, 0, 2)
    i, j = np.arange(P)[:, None], np.arange(P)[None, :]
    c = np.zeros((P, NCONST), np.float32)
    c[:, C_ID:C_ID + P] = i == j
    c[:, C_TRI:C_TRI + P] = i <= j
    c[:, C_BLK:C_BLK + P] = (i % H1) == (j // DH)
    c[:, C_SEG:C_SEG + P] = (j % H1) != 0
    c[:, C_REV:C_REV + P] = E - j % E
    c[:, C_IOTA:C_IOTA + P] = j
    c[:, C_ONES:C_ONES + P] = 1
    c[:, C_J128:C_J128 + NSLOT] = P * np.arange(NSLOT)
    kn = np.arange(NPK)[None, :]
    c[:, C_TOK:C_TOK + NPK] = (P * (kn % NT) + i + 1) * np.where(kn < NT, 1, -1)
    c[:, C_DUMMY:C_DUMMY + NSLOT] = TOPK * NTOK + P * np.arange(NSLOT) + i
    c[:, C_HALF:C_HALF + 16] = -0.5
    c[:, C_EPS] = EPS_LN
    c[:, C_NEG] = -1
    cb = np.zeros((P, NCONSTB), np.float32)
    cb[:, B_ID:B_ID + P] = i == j
    cb[:, B_STRICT:B_STRICT + P] = i < j
    cb[:, B_ONE:B_ONE + P] = 1
    cb[:, B_MASK:B_MASK + HM] = np.where(np.arange(HM)[None, :] % M > i, -BIG, 0)
    return {
        "xn": x, "xT": x.T, "wqkv": wqkv, "wo1": a["L0_attn_Wo"], "bo1": a["L0_attn_bo"].reshape(D),
        "consts": c, "constb": cb.astype(mybir.dt.np(BF16)), "ctxT": a["ctx_1024"].reshape(BM, D).T,
        "wk": pairs(a["L0_xattn_Wk"]), "wv": pairs(a["L0_xattn_Wv"]),
        "wqT": pairs(a["L0_xattn_Wq"]).T.reshape(NPAIR, P, D).transpose(1, 0, 2), "biases": biases,
        "wo2": pairs(a["L0_xattn_Wo"].T).T.reshape(NPAIR, P, D).transpose(1, 0, 2), "router": a["L0_ffn_router_w"],
        "wgu": wgu.reshape(D, E * 2 * FP), "wdn": wdn.reshape(P, E * NF * D),
    }


def kernel(**inputs):
    import numpy as np
    import concourse.bacc as bacc
    from concourse.bass_utils import run_bass_kernel_spmd

    nc = bacc.Bacc("TRN2", target_bir_lowering=False, num_devices=1)
    arrays, args = {}, []
    for name, value in layout(inputs).items():
        value = np.ascontiguousarray(value)
        arrays[f"in_{name}"] = value
        args.append(nc.dram_tensor(f"in_{name}", value.shape, mybir.dt.from_np(value.dtype), kind="ExternalInput").ap())
    out = nc.dram_tensor("out_rows", (NTOK, D), F32, kind="ExternalOutput").ap()
    decoder_layer(nc, *args, out)
    r = run_bass_kernel_spmd(nc, [arrays], core_ids=[0])
    return r.results[0]["out_rows"].reshape(B, T, D)
```

```python
from contextlib import ExitStack

import concourse.bass as bass
from concourse import mybir

F32 = mybir.dt.float32
BF16 = mybir.dt.bfloat16
F16 = mybir.dt.float16
I32 = mybir.dt.int32
ALU = mybir.AluOpType
ACT = mybir.ActivationFunctionType
AX = mybir.AxisListType

P = 128
B, T, D = 4, 512, 128
NTOK = B * T
NT = NTOK // P
TPB = T // P
H1, DH = 16, 8
H2, DX, M = 16, 64, 32
HM = H2 * M
BM = B * M
NPAIR = H2 // 2
KT4 = HM // P
E, F = 8, 352
NF = -(-F // P)
FP = NF * P
TOPK = 2
NPK = TOPK * NT
NSLOT = TOPK * NTOK // P + E - 1
UNR = 3
NIT = NSLOT // UNR
EPS_Z = 1e-6
EPS_LN = 1e-5
BIG = 1e30
assert NIT * UNR == NSLOT

C_ID = 0
C_TRI = C_ID + P
C_BLK = C_TRI + P
C_SEG = C_BLK + P
C_REV = C_SEG + P
C_IOTA = C_REV + P
C_ONES = C_IOTA + P
C_J128 = C_ONES + P
C_TOK = C_J128 + NSLOT
C_DUMMY = C_TOK + NPK
C_HALF = C_DUMMY + NSLOT
C_EPS = C_HALF + 16
C_NEG = C_EPS + 1
NCONST = C_NEG + 1
Z_BANK = (None, None, 5, 5, 6, 6, 7, 2)
NACT = 10
ROW_CHUNKS = ((10, 18), (18, 26), (26, 32))
VWT_BANK = (1, 2, 4, 5)
VW_BANK = (6, 7, 1, 2)
B_ID, B_STRICT, B_ONE, B_MASK = 0, P, 2 * P, 3 * P
NCONSTB = B_MASK + HM

SEMS = """ld_x0 ld_x1 ld_wqkv ld_wo1 ld_router ld_const ld_tables ld_constb ld_ctx ld_wk ld_wv ld_wq ld_bias ld_wo2 ld_gu ld_dn ld_bo1
 kt_ps vt_ps kt_sb vt_sb g_ps g_sb c_ps c_hi c_r1 c_mid c_r2 c_split csT_ps csT_sb crow_zero crow_ld
 vwt_ps vwt_sb vw_ps vw_sb xb_ready
 qkv_ps er_ready v_ready feat kc_ready kq_ready den_ready z_ready kv_ready u0_ps u1_ps qu_ready intra_ready
 s_ps sblk_ready qt_ps qt_sb inter_ps comb_ready out_ready outT_ps oT_sb wo_ps y1_ready st1_ready var1_ready
 ve1_ready rs1_ready nb1_ready x1_ready x1t_ps x1t_sb sc_ps max_ready sd_ready exp_ready sum_ready rsm_ready pn_ready
 pt_ps pt_sb pv_ps y2_ready st2_ready var2_ready ve2_ready rs2_ready nb2_ready x2_ready x2_ld x2t_ps x2t_sb rt_ps
 logits_ready route e2_ready onehot_ready rank_ps rowf_ready tile_eq tilesel_ready absd_ready rowsel_act rowsel_ready slot_ps src_ready texp_ready dst_ready xgt_ps xgt_sb
 wb_ready gate_ps up_ps silu_ready a_ready down_ps y_ready diag_ready z_first z_sum0 z_sum z_st dl_ready z_var z_ve z_rs z_nb zn_ready zn_last out_st""".split()


def decoder_layer(nc, xn, xT, wqkv, wo1, bo1, consts, constb, ctxT, wk, wv, wqT, biases, wo2, router,
                  wgu, wdn, out):
    x2_dram = nc.dram_tensor("x2_rows", (NTOK, D), F32, kind="Internal").ap()
    y_dram = nc.dram_tensor("expert_rows", (TOPK * NTOK + NSLOT * P, D), F32, kind="Internal").ap()

    with ExitStack() as ctx:
        def sb(name, shape, dt=F32):
            return ctx.enter_context(nc.sbuf_tensor(name, shape, dt))

        S = {n: ctx.enter_context(nc.semaphore(n)) for n in SEMS}
        xt_loaded = [ctx.enter_context(nc.semaphore(f"xt_loaded{c}")) for c in range(TPB)]
        x2_stored = [ctx.enter_context(nc.semaphore(f"x2_stored{c}")) for c in range(TPB)]
        y_ld = [ctx.enter_context(nc.semaphore(f"y_ld{g}")) for g in range(4)]
        xg_loaded = [ctx.enter_context(nc.semaphore(f"xg_loaded{c}")) for c in range(UNR)]
        y_scattered = [ctx.enter_context(nc.semaphore(f"y_scattered{c}")) for c in range(UNR)]

        c32 = sb("c32", [P, NCONST])
        cb = sb("cb", [P, NCONSTB], BF16)
        wqkv_sb = sb("wqkv_sb", [P, 3 * D])
        wo1_sb = sb("wo1_sb", [P, D])
        bo1_sb = sb("bo1_sb", [P, D])
        router_sb = sb("router_sb", [P, E])
        wgu_sb = sb("wgu_sb", [P, E * 2 * FP])
        wdn_sb = sb("wdn_sb", [P, E * NF * D])
        ident, tri = c32[:, C_ID:C_ID + P], c32[:, C_TRI:C_TRI + P]
        blockmask, segment = c32[:, C_BLK:C_BLK + P], c32[:, C_SEG:C_SEG + P]
        identb, strictb, onesb = cb[:, B_ID:B_ID + P], cb[:, B_STRICT:B_STRICT + P], cb[:, B_ONE:B_ONE + P]
        causalb = cb[:, B_MASK:B_MASK + HM]
        ctx_sb = sb("ctx_sb", [P, BM])
        early = sb("early", [P, 8 * H2 * DX])
        part = lambda k, n=1: early[:, k * H2 * DX:(k + n) * H2 * DX]
        wk_sb, wv_sb = part(0), part(1)
        wq_sb = part(2).rearrange("p (q d) -> p q d", q=NPAIR)
        wo2_sb = part(3).rearrange("p (q d) -> p q d", q=NPAIR)
        kT = part(4).rearrange("p (q m) -> p q m", q=NPAIR)
        vT = part(5).rearrange("p (q m) -> p q m", q=NPAIR)
        vwT = part(6, 2).rearrange("p (b m) -> p b m", b=B)
        yk = part(0, 4).rearrange("p (k n d) -> p k n d", k=TOPK, d=D)
        z0 = part(4)[:, 0:4 * D].rearrange("p (n d) -> p n d", d=D)
        zn = part(6, 2).rearrange("p (n d) -> p n d", d=D)
        bias_sb = sb("bias_sb", [P, 2 * NPAIR + H2 + 1])
        G = sb("G", [P, B, HM])
        VW = sb("VW", [P, B, KT4 * D])
        c_r = sb("c_r", [P, 2, H2])
        c_parts = sb("c_parts", [P, 3, H2], BF16)
        c_partsT = sb("c_partsT", [H2, 3, BM], BF16)
        crow = sb("crow", [P, H2, BM], BF16)
        x_all = sb("x_all", [P, NT, D])
        xb_all = sb("xb_all", [P, NT, D])
        diag = (x_all, xb_all)
        xT_sb = sb("xT_sb", [P, TPB, P])
        ex = sb("ex", [P, 2, 2 * D])
        rl = sb("rl", [P, 2, 2 * D])
        vn = sb("vn", [P, 2, D])
        qk = sb("qk", [P, 2, 2 * D])
        kcum = sb("kcum", [P, D])
        kcq = sb("kcq", [P, D + H1])
        den = sb("den", [P, H1])
        Z = sb("Z", [P, H1])
        kv = sb("kv", [P, 2, DH * D])
        qu = sb("qu", [P, DH * D])
        intra = sb("intra", [P, D])
        osum = sb("osum", [P, D])
        on_t = sb("on_t", [P, D])
        sblk = sb("sblk", [P, D])
        qT = sb("qT", [P, P])
        oT = sb("oT", [P, P])
        y1 = sb("y1", [P, 2, D])
        st = sb("st", [P, 2, 6])
        mv1 = sb("mv1", [P, 2, 2])
        ve = sb("ve", [P, 4])
        negm = sb("negm", [P, 4])
        nb1 = sb("nb1", [P, 2])
        nb2 = sb("nb2", [P, 2])
        rs1 = sb("rs1", [P, 2])
        x1 = sb("x1", [P, TPB, D])
        x1T = sb("x1T", [P, P])
        mx = sb("mx", [P, H2])
        pr = sb("pr", [P, 2, HM])
        sm = sb("sm", [P, H2])
        rsm = sb("rsm", [P, 2, H2])
        pn = sb("pn", [P, 2, HM])
        pT = sb("pT", [P, HM])
        y2 = sb("y2", [P, 2, D])
        mv2 = sb("mv2", [P, 2, 2])
        rs2 = sb("rs2", [P, 2])
        x2_ring = sb("x2_ring", [P, TPB, D])
        x2_all = sb("x2_all", [P, NT, D])
        x2T = sb("x2T", [P, P])
        logits = sb("logits", [P, NT, E])
        top = sb("top", [P, TOPK, NT])
        eq = sb("eq", [P, NT, E])
        cand = sb("cand", [P, NT, E])
        pick = sb("pick", [P, NT])
        onehot = sb("onehot", [P, TOPK, NT, E])
        l2nd = sb("l2nd", [P, NT, E])
        hotb = sb("hotb", [P, NT, E], BF16)
        dl = sb("dl", [P, NT])
        e2 = sb("e2", [P, NT])
        wtop = sb("wtop", [P, TOPK, NT])
        tot = sb("tot", [P, E, NT])
        cnt = sb("cnt", [P, E])
        cnti = sb("cnti", [P, E], I32)
        pad = sb("pad", [P, E])
        scan = sb("scan", [P, E, NT])
        base = sb("base", [P, E, NT])
        pos = sb("pos", [P, NT, E])
        posk = sb("posk", [P, TOPK, NT, E])
        sloti = sb("sloti", [P, NPK], I32)
        rowi = sb("rowi", [P, 2, NPK], I32)
        rowf = sb("rowf", [P, 2, NPK])
        endcmp = sb("endcmp", [P, NSLOT, E])
        texp = sb("texp", [P, NSLOT])
        texpi = sb("texpi", [P, NSLOT], I32)
        absd = sb("absd", [P, NACT, P], F16)
        rowsel = sb("rowsel", [P, NPK, P], F16)
        tilesel = sb("tilesel", [P, NPK, NSLOT], F16)
        sv = sb("sv", [P, 4, NSLOT])
        src_row = sb("src_row", [P, NSLOT], I32)
        dst_row = sb("dst_row", [P, NSLOT], I32)
        xg = sb("xg", [P, UNR, D])
        xgT = sb("xgT", [P, UNR, P])
        wb = part(4, 4)[:, 0:UNR * 2 * FP].rearrange("p (u f) -> p u f", u=UNR)
        sg = sb("sg", [P, UNR, FP])
        aT = sb("aT", [P, UNR, FP])
        yx = sb("yx", [P, UNR, D])
        stz = sb("stz", [P, NT, 6])
        mvz = sb("mvz", [P, NT, 2])
        vez = sb("vez", [P, NT])
        rsz = sb("rsz", [P, NT])
        negz = sb("negz", [P, NT])
        nbz = sb("nbz", [P, NT])

        ps = [ctx.enter_context(nc.psum_tensor(f"bank{i}", [P, 512], F32)) for i in range(8)]
        z_of = lambda t: z0[:, t, :] if t < 4 else ps[Z_BANK[t // 2]][:, t % 4 * D:(t % 4 + 1) * D]
        block = ctx.enter_context(nc.Block())

        def tile_steps(eng, step, lag):
            for c in range(TPB):
                step(0, c)
            with eng.Fori(1, B) as b:
                for c in range(TPB):
                    step(b, c)
            for c in range(lag):
                step(B, c)

        def on(b, c, lag):
            return not isinstance(b, int) or 0 <= TPB * b + c - lag < NT

        def cnt_of(b, c, lag):
            return TPB * b + (c - lag + 1)

        def carries(b, c, lag):
            k = c - lag
            return 3 * (b + k // TPB) + k % TPB

        def wait(eng, sem, v):
            if not isinstance(v, int) or v > 0:
                eng.wait_ge(sem, v)

        @block.sync
        def _(sp):
            x_rows = xn.rearrange("(n p) d -> p n d", p=P)
            sp.dma_start(xT_sb[:, 0, :], xT[:, 0:P]).then_inc(xt_loaded[0], 16)
            sp.dma_start(wqkv_sb[:], wqkv).then_inc(S["ld_wqkv"], 16)
            sp.dma_start(ctx_sb[:], ctxT).then_inc(S["ld_ctx"], 16)
            sp.dma_start(wk_sb, wk).then_inc(S["ld_wk"], 16)
            sp.dma_start(c32[:, 0:C_REV], consts[:, 0:C_REV]).then_inc(S["ld_const"], 16)
            sp.dma_start(bias_sb[:], biases).then_inc(S["ld_bias"], 16)
            sp.dma_start(wv_sb, wv).then_inc(S["ld_wv"], 16)
            sp.dma_start(wq_sb, wqT).then_inc(S["ld_wq"], 16)
            sp.dma_start(cb[:], constb).then_inc(S["ld_constb"], 16)
            sp.dma_start(wo2_sb, wo2).then_inc(S["ld_wo2"], 16)
            sp.dma_start(xT_sb[:, 1, :], xT[:, P:2 * P]).then_inc(xt_loaded[1], 16)
            sp.dma_start(wo1_sb[:], wo1).then_inc(S["ld_wo1"], 16)
            sp.dma_start(bo1_sb[:], bo1.partition_broadcast(P)).then_inc(S["ld_bo1"], 16)
            sp.dma_start(x_all[:, 0:TPB, :], x_rows[:, 0:TPB, :]).then_inc(S["ld_x0"], 16)
            sp.dma_start(c32[:, C_REV:NCONST], consts[:, C_REV:NCONST]).then_inc(S["ld_tables"], 16)
            for c in range(2, TPB):
                sp.dma_start(xT_sb[:, c, :], xT[:, c * P:(c + 1) * P]).then_inc(xt_loaded[c], 16)
            sp.dma_start(router_sb[:], router).then_inc(S["ld_router"], 16)
            sp.dma_start(x_all[:, TPB:, :], x_rows[:, TPB:, :]).then_inc(S["ld_x1"], 16)
            sp.wait_ge(S["csT_sb"], 1)
            sp.wait_ge(S["crow_zero"], 1)
            for k in range(3):
                sp.dma_start(crow[k:k + 1], c_partsT[:, k, :]).then_inc(S["crow_ld"], 16)
            sp.dma_start(wgu_sb[:], wgu).then_inc(S["ld_gu"], 16)
            sp.dma_start(wdn_sb[:], wdn).then_inc(S["ld_dn"], 16)

            def step(b, c):
                if not isinstance(b, int) or b < B - 1:
                    sp.wait_ge(S["qkv_ps"], cnt_of(b, c, 0))
                    sp.dma_start(xT_sb[:, c, :], xT[:, bass.ds((b + 1) * T + c * P, P)]).then_inc(xt_loaded[c], 16)
                if on(b, c, 4):
                    sp.wait_ge(S["x2_ready"], cnt_of(b, c, 4))
                    sp.dma_start(x2_dram[bass.ds((b - 1) * T + c * P, P), :],
                                 x2_ring[:, c, :]).then_inc(x2_stored[c], 16)

            for c in range(TPB):
                step(0, c)
            with sp.Fori(1, B - 1) as b:
                for c in range(TPB):
                    step(b, c)
            for b in (B - 1, B):
                for c in range(TPB):
                    step(b, c)
            for c in range(TPB):
                sp.wait_ge(x2_stored[c], 16 * (B + 1))
            sp.dma_start(x2_all[:], x2_dram.rearrange("(n p) d -> p n d", p=P)).then_inc(S["x2_ld"], 16)
            for k in range(UNR):
                sp.wait_ge(y_scattered[k], 16 * NIT)
            yv = y_dram[0:TOPK * NTOK, :].rearrange("(k n p) d -> p k n d", p=P, k=TOPK)
            for g in range(4):
                for k in range(TOPK):
                    sp.dma_start(yk[:, k, 4 * g:4 * g + 4, :], yv[:, k, 4 * g:4 * g + 4, :]).then_inc(y_ld[g], 16)
            ov = out.rearrange("(n p) d -> p n d", p=P)
            for g in range(4):
                if g != 2:
                    sp.wait_ge(S["zn_ready"], min(g + 1, 3))
                if g >= 2:
                    sp.wait_ge(S["zn_last"], g - 1)
                sp.dma_start(ov[:, 4 * g:4 * g + 4, :], zn[:, 4 * g:4 * g + 4, :]).then_inc(S["out_st"], 16)
            sp.wait_ge(S["out_st"], 64)

        @block.tensor
        def _(pe):
            mm = nc.tensor.matmul

            def context_products():
                pe.wait_ge(S["ld_ctx"], 16)
                for w, bank, loaded, done in ((wk_sb, 4, "ld_wk", "kt_ps"), (wv_sb, 6, "ld_wv", "vt_ps")):
                    pe.wait_ge(S[loaded], 16)
                    for q in range(NPAIR):
                        last = mm(ps[bank + q // 4][:, (q % 4) * BM:(q % 4 + 1) * BM], w[:, q * P:(q + 1) * P],
                                  ctx_sb[:], start=True, stop=True)
                    last.then_inc(S[done], 1)
                pe.wait_ge(S["kt_sb"], 1)
                for q in range(NPAIR):
                    last = mm(ps[3][:, 2 * q:2 * q + 2], kT[:, q, :],
                              bias_sb[:, 2 * NPAIR + 2 * q:2 * NPAIR + 2 * q + 2], start=True, stop=True)
                last.then_inc(S["c_ps"], 1)

                def head_products(h, bank, w, t, done):
                    r = slice(DX * (h // NPAIR), DX * (h // NPAIR) + DX)
                    last = mm(ps[bank][:, (h % 4) * BM:(h % 4 + 1) * BM], w[r, h % NPAIR, :], t[r, h % NPAIR, :],
                              start=True, stop=True)
                    if h % 4 == 3:
                        last.then_inc(S[done], 1)

                pe.wait_ge(S["ld_wq"], 16)
                for h in range(H2):
                    if h == 8:
                        pe.wait_ge(S["vt_sb"], 1)
                    head_products(h, 4 + h // 4, wq_sb, kT, "g_ps")
                pe.wait_ge(S["c_split"], 1)
                pe.wait_ge(S["ld_constb"], 16)
                for t in range(3):
                    last = nc.tensor.transpose(ps[3].bitcast(BF16)[0:H2, t * BM:(t + 1) * BM], c_parts[:, t, :], identb)
                last.then_inc(S["csT_ps"], 1)
                pe.wait_ge(S["ld_wo2"], 16)
                for h in range(H2):
                    if h >= 8 and h % 4 == 0:
                        pe.wait_ge(S["g_sb"], h // 4 - 1)
                    head_products(h, VWT_BANK[h // 4], wo2_sb, vT, "vwt_ps")
                pe.wait_ge(S["vwt_sb"], 4)
                pe.wait_ge(S["ld_const"], 16)
                for b in range(B):
                    if b < 2:
                        pe.wait_ge(S["g_sb"], b + 3)
                    for t in range(KT4):
                        last = nc.tensor.transpose(ps[VW_BANK[b]][:, t * D:(t + 1) * D], vwT[:, b, t * P:(t + 1) * P], ident)
                    last.then_inc(S["vw_ps"], 1)
                pe.wait_ge(S["vw_sb"], 4)
                pe.wait_ge(S["csT_sb"], 1)

            def step(b, c):
                n = lambda lag: cnt_of(b, c, lag)
                carried = c > 0
                batch = lambda lag: b + (c - lag) // TPB
                row = lambda t, bb: t[:, bb, :] if isinstance(bb, int) else t[:, bass.ds(bb, 1), :]
                first_batch = isinstance(b, int) and b == 0
                if on(b, c, 0):
                    if first_batch and c == 0:
                        pe.wait_ge(S["ld_wqkv"], 16)
                    if first_batch and c == 1:
                        pe.wait_ge(S["ld_wo1"], 16)
                    pe.wait_ge(xt_loaded[c], 16 * (b + 1))
                    mm(ps[0][:, 0:3 * D], xT_sb[:, c, :], wqkv_sb[:], start=True, stop=True).then_inc(S["qkv_ps"], 1)
                if on(b, c, 2):
                    pe.wait_ge(S["x1_ready"], n(2))
                    wait(pe, S["logits_ready"], n(5))
                    nc.tensor.transpose(ps[4][:, 2 * P:3 * P], x1[:, (c - 2) % TPB, :], ident).then_inc(S["x1t_ps"], 1)
                if on(b, c, 3):
                    pe.wait_ge(S["pn_ready"], n(3))
                    wait(pe, S["y2_ready"], n(4))
                    s2 = (c - 3) % 2
                    for k in range(KT4):
                        last = nc.tensor.transpose(ps[6][:, k * P:(k + 1) * P], pn[:, s2, k * P:(k + 1) * P], ident)
                    last.then_inc(S["pt_ps"], 1)
                if on(b, c, 2):
                    pe.wait_ge(S["x1t_sb"], n(2))
                    if first_batch and c == 2:
                        pe.wait_ge(S["g_sb"], 4)
                        pe.wait_ge(S["crow_ld"], 3 * 16)
                    bb = batch(2)
                    first = (c - 2) % TPB == 0
                    mm(ps[5][:], x1T[:], row(G, bb), start=True, stop=False)
                    last = mm(ps[5][:].rearrange("p (h m) -> p h m", m=M), onesb, crow[:, :, bass.ds(bb * M, M)],
                              start=False, stop=not first)
                    if first:
                        last = mm(ps[5][:], identb, causalb, start=False, stop=True)
                    last.then_inc(S["sc_ps"], 1)
                if on(b, c, 1):
                    pe.wait_ge(S["out_ready"], n(1))
                    nc.tensor.transpose(ps[7][:, 0:P], on_t[:], ident).then_inc(S["outT_ps"], 1)
                if on(b, c, 3):
                    pe.wait_ge(S["pt_sb"], n(3))
                    bb = batch(3)
                    for k in range(KT4):
                        last = mm(ps[6][:, 0:D], pT[:, k * P:(k + 1) * P], VW[:, bb, k * D:(k + 1) * D]
                                  if isinstance(bb, int) else VW[:, bass.ds(bb, 1), k * D:(k + 1) * D],
                                  start=k == 0, stop=k == KT4 - 1)
                    last.then_inc(S["pv_ps"], 1)
                if on(b, c, 4):
                    pe.wait_ge(S["x2_ready"], n(4))
                    if not on(b, c, 2):
                        wait(pe, S["logits_ready"], n(5))
                    nc.tensor.transpose(ps[4][:, 0:P], x2_ring[:, c, :], ident).then_inc(S["x2t_ps"], 1)
                if on(b, c, 1):
                    pe.wait_ge(S["oT_sb"], n(1))
                    mm(ps[7][:, P:P + D], oT[:], wo1_sb[:], start=True, stop=True).then_inc(S["wo_ps"], 1)
                if on(b, c, 0) and carried:
                    pe.wait_ge(S["feat"], n(0))
                    pe.wait_ge(S["v_ready"], n(0))
                    nc.tensor.transpose(ps[0][:, 0:P], qk[:, c % 2, 0:D], ident).then_inc(S["qt_ps"], 1)
                if on(b, c, 4):
                    pe.wait_ge(S["x2t_sb"], n(4))
                    mm(ps[4][:, P:P + E], x2T[:], router_sb[:], start=True, stop=True).then_inc(S["rt_ps"], 1)
                def running_sum(k):
                    mm(ps[1 + k][:], tri, kv[:, c % 2, k * 512:(k + 1) * 512], start=True,
                       stop=True).then_inc(S[f"u{k}_ps"], 1)
                if first_batch and c == 0:
                    context_products()
                if on(b, c, 0):
                    pe.wait_ge(S["kv_ready"], n(0))
                    running_sum(0)
                if on(b, c, 0):
                    running_sum(1)
                if on(b, c, 0) and carried:
                    pe.wait_ge(S["qt_sb"], carries(b, c, 0))
                    wait(pe, S["y1_ready"], n(1))
                    mm(ps[7][:, 2 * P:2 * P + D], qT[:], sblk[:], start=True, stop=True).then_inc(S["inter_ps"], 1)
                if on(b, c, 0) and c < TPB - 1:
                    if not carried:
                        wait(pe, S["sblk_ready"], carries(b, c, 0))
                    mm(ps[3][:, 0:D], qk[:, c % 2, D:2 * D], vn[:, c % 2, :], start=c == 0, stop=True,
                       skip_group_check=True).then_inc(S["s_ps"], 1)
                if first_batch and c == 3:
                    pe.wait_ge(S["ld_router"], 16)

            tile_steps(pe, step, 4)

            pe.wait_ge(S["onehot_ready"], 1)
            hb = hotb[:].rearrange("p n e -> p (n e)")
            mm(ps[0][:, 0:P], strictb, hb, start=True, stop=True)
            mm(ps[0][:, P:2 * P], onesb, hb, start=True, stop=True).then_inc(S["rank_ps"], 1)
            pe.wait_ge(S["tilesel_ready"], 1)
            for (lo, hi), sem, count in ((ROW_CHUNKS[0], "rowsel_ready", 1), (ROW_CHUNKS[1], "rowsel_ready", 2),
                                         ((0, NACT), "rowsel_act", 1), (ROW_CHUNKS[2], "rowsel_ready", 3)):
                pe.wait_ge(S[sem], count)
                for i in range(lo, hi):
                    last = mm(ps[1][:, 0:NSLOT], rowsel[:, i, :], tilesel[:, i, :], start=i == NACT, stop=i == NPK - 1)
            last.then_inc(S["slot_ps"], 1)
            pe.wait_ge(S["texp_ready"], 1)
            pe.wait_ge(S["ld_gu"], 16)
            pe.wait_ge(S["ld_dn"], 16)

            def estep(i, u):
                has = lambda lag: not isinstance(i, int) or 0 <= UNR * i + u - lag < NSLOT
                n = lambda lag: UNR * i + (u - lag + 1)
                sl = lambda lag: (u - lag) % UNR
                if has(1):
                    pe.wait_ge(S["wb_ready"], n(1))
                    pe.wait_ge(S["xgt_sb"], n(1))
                    wait(pe, S["silu_ready"], n(2))
                    for k in range(NF):
                        last = mm(ps[0][:, k * P:(k + 1) * P], wb[:, sl(1), k * P:(k + 1) * P], xgT[:, sl(1), :],
                                  start=True, stop=True)
                    last.then_inc(S["gate_ps"], 1)
                if has(0):
                    pe.wait_ge(xg_loaded[u], 16 * (i + 1))
                    wait(pe, S["xgt_sb"], n(1))
                    nc.tensor.transpose(ps[4][:, 0:P], xg[:, u, :], ident).then_inc(S["xgt_ps"], 1)
                if has(1):
                    wait(pe, S["a_ready"], n(2))
                    for k in range(NF):
                        last = mm(ps[1][:, k * P:(k + 1) * P], wb[:, sl(1), FP + k * P:FP + (k + 1) * P],
                                  xgT[:, sl(1), :], start=True, stop=True)
                    last.then_inc(S["up_ps"], 1)
                if has(2):
                    ed = pe.value_load(texpi[0:1, bass.ds(UNR * i + (u - 2), 1)], min_val=0, max_val=E - 1)
                    pe.wait_ge(S["a_ready"], n(2))
                    wait(pe, S["y_ready"], n(3))
                    for k in range(NF):
                        last = mm(ps[3][:, 0:D], aT[:, sl(2), k * P:(k + 1) * P],
                                  wdn_sb[:, bass.ds(ed * (NF * D) + k * D, D)], start=k == 0, stop=k == NF - 1)
                    last.then_inc(S["down_ps"], 1)

            for i in range(2):
                for u in range(UNR):
                    estep(i, u)
            with pe.Fori(2, NIT) as i:
                for u in range(UNR):
                    estep(i, u)
            for u in range(3):
                estep(NIT, u)

            pe.wait_ge(y_scattered[UNR - 1], 16 * NIT)
            pe.wait_ge(S["x2_ld"], 16)
            for lo, hi in ((4, 8), (8, 12), (12, 14), (14, 16)):
                mm(ps[Z_BANK[lo // 2]][:, lo % 4 * D:(lo % 4 + hi - lo) * D], ident,
                   x2_all[:, lo:hi, :].rearrange("p n d -> p (n d)"), start=True, stop=False)
            for q in range(1, 4):
                if q == 1:
                    pe.wait_ge(S["diag_ready"], 4)
                pe.wait_ge(y_ld[q], 32)
                for t in range(4 * q, 4 * q + 4):
                    for k in range(TOPK):
                        last = mm(z_of(t), diag[k][:, t, :], yk[:, k, t, :], start=False,
                                  stop=t in (7, 11, 13, 15) and k == TOPK - 1)
                last.then_inc(S["z_sum"], 1)

        @block.scalar
        def _(ac):
            act_f = nc.scalar.activation

            def context_copies():
                for g in range(4):
                    ac.wait_ge(S["g_ps"], g + 1)
                    act_f(G[:, :, g * P:(g + 1) * P].rearrange("p b (h m) -> p h b m", m=M),
                          ps[4 + g][:].rearrange("p (h b m) -> p h b m", b=B, m=M), ACT.Copy).then_inc(S["g_sb"], 1)
                ac.wait_ge(S["csT_ps"], 1)
                act_f(c_partsT[:].rearrange("p k m -> p (k m)"), ps[3].bitcast(BF16)[0:H2, 0:3 * BM],
                      ACT.Copy).then_inc(S["csT_sb"], 1)
                for b in range(B):
                    ac.wait_ge(S["vw_ps"], b + 1)
                    act_f(VW[:, b, :], ps[VW_BANK[b]][:], ACT.Copy).then_inc(S["vw_sb"], 1)

            def step(b, c):
                n = lambda lag: cnt_of(b, c, lag)
                if on(b, c, 0):
                    s2 = c % 2
                    ac.wait_ge(S["qkv_ps"], n(0))
                    act_f(ex[:, s2, :], ps[0][:, 0:2 * D], ACT.Exp)
                    act_f(rl[:, s2, :], ps[0][:, 0:2 * D], ACT.Relu).then_inc(S["er_ready"], 1)
                if on(b, c, 2):
                    ac.wait_ge(S["x1t_ps"], n(2))
                    act_f(x1T[:], ps[4][:, 2 * P:3 * P], ACT.Copy).then_inc(S["x1t_sb"], 1)
                if on(b, c, 0):
                    act_f(vn[:, c % 2, :], ps[0][:, 2 * D:3 * D], ACT.Copy).then_inc(S["v_ready"], 1)
                if on(b, c, 3):
                    ac.wait_ge(S["pt_ps"], n(3))
                    act_f(pT[:], ps[6][:], ACT.Copy).then_inc(S["pt_sb"], 1)
                if on(b, c, 4):
                    ac.wait_ge(S["nb2_ready"], n(4))
                    ac.wait_ge(x2_stored[c], 16 * b)
                    act_f(x2_ring[:, c, :], y2[:, c % 2, :], ACT.Identity, bias=nb2[:, c % 2:c % 2 + 1],
                          scale=rs2[:, c % 2:c % 2 + 1]).then_inc(S["x2_ready"], 1)
                if on(b, c, 1):
                    ac.wait_ge(S["outT_ps"], n(1))
                    act_f(oT[:], ps[7][:, 0:P], ACT.Copy).then_inc(S["oT_sb"], 1)
                if on(b, c, 4):
                    ac.wait_ge(S["x2t_ps"], n(4))
                    act_f(x2T[:], ps[4][:, 0:P], ACT.Copy).then_inc(S["x2t_sb"], 1)
                if on(b, c, 0) and c > 0:
                    ac.wait_ge(S["qt_ps"], carries(b, c, 0))
                    act_f(qT[:], ps[0][:, 0:P], ACT.Copy).then_inc(S["qt_sb"], 1)
                if on(b, c, 2):
                    ac.wait_ge(S["sd_ready"], n(2))
                    act_f(pr[:, c % 2, :], pr[:, c % 2, :], ACT.Exp, scale=float(DX) ** -0.5).then_inc(S["exp_ready"], 1)
                if on(b, c, 1):
                    s2 = (c - 1) % 2
                    ac.wait_ge(S["nb1_ready"], n(1))
                    act_f(x1[:, (c - 1) % TPB, :], y1[:, s2, :], ACT.Identity, bias=nb1[:, s2:s2 + 1],
                          scale=rs1[:, s2:s2 + 1]).then_inc(S["x1_ready"], 1)
                if isinstance(b, int) and b == 0 and c == 0:
                    context_copies()

            tile_steps(ac, step, 4)
            ac.wait_ge(S["dl_ready"], 1)
            act_f(e2[:], dl[:], ACT.Exp).then_inc(S["e2_ready"], 1)
            ac.preload_act_table_set("silu_and_others")
            ac.wait_ge(S["rowf_ready"], 1)
            for i in range(NACT):
                last = act_f(absd[:, i, :], c32[:, C_IOTA:C_IOTA + P], ACT.Abs, bias=rowf[:, 0, i:i + 1], scale=-1.0)
            last.then_inc(S["absd_ready"], 1)
            ac.wait_ge(S["absd_ready"], 1)
            act_f(rowsel[:, 0:NACT, :], absd[:], ACT.Relu, bias=c32[:, C_ONES:C_ONES + 1], scale=-1.0
                  ).then_inc(S["rowsel_act"], 1)

            ac.wait_ge(S["texp_ready"], 1)
            ac.wait_ge(S["ld_gu"], 16)

            def estep(i, u):
                has = lambda lag: not isinstance(i, int) or 0 <= UNR * i + u - lag < NSLOT
                n = lambda lag: UNR * i + (u - lag + 1)
                if has(0):
                    e = ac.value_load(texpi[0:1, bass.ds(UNR * i + u, 1)], min_val=0, max_val=E - 1)
                    act_f(wb[:, u, :], wgu_sb[:, bass.ds(e * (2 * FP), 2 * FP)], ACT.Copy).then_inc(S["wb_ready"], 1)
                if has(1):
                    ac.wait_ge(S["gate_ps"], n(1))
                    wait(ac, S["a_ready"], n(4))
                    act_f(sg[:, (u - 1) % UNR, :], ps[0][:, 0:FP], ACT.Silu).then_inc(S["silu_ready"], 1)
                if has(0):
                    ac.wait_ge(S["xgt_ps"], n(0))
                    wait(ac, S["up_ps"], UNR * i + u - UNR + 1)
                    act_f(xgT[:, u, :], ps[4][:, 0:P], ACT.Copy).then_inc(S["xgt_sb"], 1)

            for i in range(2):
                for u in range(UNR):
                    estep(i, u)
            with ac.Fori(2, NIT) as i:
                for u in range(UNR):
                    estep(i, u)
            for u in range(3):
                estep(NIT, u)

            for q in (0, 1, 3):
                ac.wait_ge(S["z_nb"], q + 1)
                for t in range(4 * q, 4 * q + (4 if q < 3 else 2)):
                    last = act_f(zn[:, t, :], z_of(t), ACT.Identity, bias=nbz[:, t:t + 1], scale=rsz[:, t:t + 1])
                last.then_inc(S["zn_ready"], 1)

        @block.gpsimd
        def _(pool):
            g = nc.gpsimd
            g.memset(crow[:], 0.0).then_inc(S["crow_zero"], 1)

            def first_residual(k, lo, hi):
                pool.wait_ge(S[f"ld_x{k}"], 16)
                pool.wait_ge(S["ld_bo1"], 16)
                g.tensor_tensor(xb_all[:, lo:hi, :], x_all[:, lo:hi, :], bo1_sb[:].unsqueeze(1).broadcast_to([P, hi - lo, D]),
                                ALU.add).then_inc(S["xb_ready"], 1)

            half = c32[:, C_HALF:C_HALF + 1]
            eps = c32[:, C_EPS:C_EPS + 1]
            neg1 = c32[:, C_NEG:C_NEG + 1]

            def normaliser(k, mv, rs, nb, s2, n):
                pool.wait_ge(S[f"var{k}_ready"], n)
                w = 2 * (k - 1) + s2
                g.tensor_tensor(negm[:, w:w + 1], mv[:, s2, 0:1], neg1, ALU.mult)
                g.tensor_tensor(ve[:, w:w + 1], mv[:, s2, 1:2], eps, ALU.add).then_inc(S[f"ve{k}_ready"], 1)
                pool.wait_ge(S[f"ve{k}_ready"], n)
                g.tensor_tensor(rs[:, s2:s2 + 1], ve[:, w:w + 1], half, ALU.pow).then_inc(S[f"rs{k}_ready"], 1)
                pool.wait_ge(S[f"rs{k}_ready"], n)
                g.tensor_tensor(nb[:, s2:s2 + 1], rs[:, s2:s2 + 1], negm[:, w:w + 1],
                                ALU.mult).then_inc(S[f"nb{k}_ready"], 1)

            def step(b, c):
                n = lambda lag: cnt_of(b, c, lag)
                if on(b, c, 0):
                    s2 = c % 2
                    pool.wait_ge(S["feat"], n(0))
                    pool.wait_ge(S["v_ready"], n(0))
                    g.tensor_tensor(kv[:, s2, :].rearrange("p (d h e) -> p d h e", d=DH, e=DH),
                                    qk[:, s2, D:2 * D].rearrange("p (d h) -> p d h", d=DH).unsqueeze(3)
                                    .broadcast_to([P, DH, H1, DH]),
                                    vn[:, s2, :].rearrange("p (h e) -> p h e", e=DH).unsqueeze(1)
                                    .broadcast_to([P, DH, H1, DH]), ALU.mult).then_inc(S["kv_ready"], 1)
                if isinstance(b, int) and b == 0 and c == 0:
                    first_residual(0, 0, TPB)
                if isinstance(b, int) and b == 0 and c == 1:
                    pool.wait_ge(S["ld_tables"], 16)
                if isinstance(b, int) and b == 0 and c == 2:
                    first_residual(1, TPB, NT)
                if on(b, c, 1):
                    normaliser(1, mv1, rs1, nb1, (c - 1) % 2, n(1))
                if on(b, c, 2):
                    s2 = (c - 2) % 2
                    pool.wait_ge(S["rsm_ready"], n(2))
                    g.tensor_tensor(pn[:, s2, :].rearrange("p (h m) -> p h m", m=M),
                                    pr[:, s2, :].rearrange("p (h m) -> p h m", m=M),
                                    rsm[:, s2, :].unsqueeze(2).broadcast_to([P, H2, M]), ALU.mult).then_inc(S["pn_ready"], 1)
                if on(b, c, 3):
                    normaliser(2, mv2, rs2, nb2, (c - 3) % 2, n(3))

            tile_steps(pool, step, 4)

            pool.wait_ge(S["tile_eq"], 1)
            token = c32[:, C_TOK:C_TOK + NPK].unsqueeze(2).broadcast_to([P, NPK, NSLOT])
            g.tensor_tensor(tilesel[:], tilesel[:], token, ALU.mult).then_inc(S["tilesel_ready"], 1)

            pool.wait_ge(S["src_ready"], 1)
            for c in range(TPB):
                pool.wait_ge(x2_stored[c], 16 * (B + 1))
            for j in range(NSLOT + 6):
                if 0 <= j - 6:
                    t = j - 6
                    if t == 0:
                        pool.wait_ge(S["dst_ready"], 1)
                    pool.wait_ge(S["y_ready"], t + 1)
                    g.indirect_dma_start(y_dram, bass.IndirectOffsetOnAxis(ap=dst_row[:, t:t + 1], axis=0),
                                         yx[:, t % UNR, :], None).then_inc(y_scattered[t % UNR], 16)
                if j < NSLOT:
                    if j >= UNR:
                        pool.wait_ge(S["xgt_ps"], j - UNR + 1)
                    g.indirect_dma_start(xg[:, j % UNR, :], None, x2_dram,
                                         bass.IndirectOffsetOnAxis(ap=src_row[:, j:j + 1], axis=0)
                                         ).then_inc(xg_loaded[j % UNR], 16)
            for q in range(4):
                pool.wait_ge(S["z_var"], q + 1)
                sl = slice(4 * q, 4 * q + 4)
                g.tensor_tensor(vez[:, sl], mvz[:, sl, 1], eps.broadcast_to([P, 4]), ALU.add).then_inc(S["z_ve"], 1)
                pool.wait_ge(S["z_ve"], q + 1)
                g.tensor_tensor(rsz[:, sl], vez[:, sl], c32[:, C_HALF:C_HALF + 4], ALU.pow)
                g.tensor_tensor(negz[:, sl], mvz[:, sl, 0], neg1.broadcast_to([P, 4]), ALU.mult).then_inc(S["z_rs"], 1)
                pool.wait_ge(S["z_rs"], q + 1)
                g.tensor_tensor(nbz[:, sl], rsz[:, sl], negz[:, sl], ALU.mult).then_inc(S["z_nb"], 1)

        @block.vector
        def _(dv):
            v = nc.vector
            TT, TS, STT = v.tensor_tensor, v.tensor_scalar, v.scalar_tensor_tensor

            def context_copies():
                dv.wait_ge(S["ld_bias"], 16)
                for t, bank, col, src, done in ((kT, 4, 0, "kt_ps", "kt_sb"), (vT, 6, NPAIR, "vt_ps", "vt_sb")):
                    dv.wait_ge(S[src], 1)
                    for i in range(2):
                        last = TT(t[:, 4 * i:4 * i + 4, :], ps[bank + i][:].rearrange("p (q m) -> p q m", q=4),
                                  bias_sb[:, col + 4 * i:col + 4 * i + 4].unsqueeze(2).broadcast_to([P, 4, BM]), ALU.add)
                    last.then_inc(S[done], 1)
                dv.wait_ge(S["c_ps"], 1)
                c_all = ps[3][:, 0:H2].rearrange("p (q t) -> p t q", t=2)
                heads = lambda t: t.rearrange("p (t q) -> p t q", t=2)
                v.tensor_copy(heads(c_parts[:, 0, :]), c_all).then_inc(S["c_hi"], 1)
                dv.wait_ge(S["c_hi"], 1)
                TT(heads(c_r[:, 0, :]), c_all, heads(c_parts[:, 0, :]), ALU.subtract).then_inc(S["c_r1"], 1)
                dv.wait_ge(S["c_r1"], 1)
                v.tensor_copy(c_parts[:, 1, :], c_r[:, 0, :]).then_inc(S["c_mid"], 1)
                dv.wait_ge(S["c_mid"], 1)
                TT(c_r[:, 1, :], c_r[:, 0, :], c_parts[:, 1, :], ALU.subtract).then_inc(S["c_r2"], 1)
                dv.wait_ge(S["c_r2"], 1)
                v.tensor_copy(c_parts[:, 2, :], c_r[:, 1, :]).then_inc(S["c_split"], 1)
                for i in range(4):
                    dv.wait_ge(S["vwt_ps"], i + 1)
                    src = ps[VWT_BANK[i]][:].rearrange("p (h b m) -> p h b m", b=B, m=M)
                    dst = vwT[:, :, i * P:(i + 1) * P].rearrange("p b (h m) -> p h b m", m=M)
                    if i == 0:
                        TS(dst[:, 0], src[:, 0], bias_sb[:, 2 * NPAIR + H2:2 * NPAIR + H2 + 1], None, ALU.add)
                        v.tensor_copy(dst[:, 1:4], src[:, 1:4]).then_inc(S["vwt_sb"], 1)
                    else:
                        v.tensor_copy(dst, src).then_inc(S["vwt_sb"], 1)

            for c in range(TPB):
                dv.sem_inc(x2_stored[c], 16)

            v.memset(kcq[:, D:D + H1], EPS_Z)

            count = [0]

            def then(ins):
                count[0] += 1
                ins.then_inc(S["route"], 1)
                dv.wait_ge(S["route"], count[0])

            def top_two(t):
                shape = [P, t.stop - t.start, E]
                rev = c32[:, C_REV:C_REV + P].rearrange("p (n e) -> p n e", e=E)[:, t]
                lane = lambda col: col.unsqueeze(2).broadcast_to(shape)
                for k in range(TOPK):
                    src = logits if k == 0 else l2nd
                    then(v.tensor_reduce(top[:, k, t], src[:, t], AX.X, ALU.max))
                    then(TT(eq[:, t], src[:, t], lane(top[:, k, t]), ALU.is_equal))
                    then(TT(cand[:, t], eq[:, t], rev, ALU.mult))
                    then(v.tensor_reduce(pick[:, t], cand[:, t], AX.X, ALU.max))
                    then(TT(onehot[:, k, t], rev, lane(pick[:, t]), ALU.is_equal))
                    if k == 0:
                        then(STT(l2nd[:, t], onehot[:, 0, t], -3e38, logits[:, t], ALU.mult, ALU.add))

            def step(b, c):
                n = lambda lag: cnt_of(b, c, lag)
                tile = lambda t, lag: t[:, bass.ds(TPB * b + (c - lag), 1), :]
                if on(b, c, 1):
                    dv.wait_ge(S["qu_ready"], n(1))
                    v.tensor_reduce(intra[:], qu[:].rearrange("p (d f) -> p f d", d=DH), AX.X, ALU.add).then_inc(S["intra_ready"], 1)
                if on(b, c, 0):
                    s2 = c % 2
                    dv.wait_ge(S["er_ready"], n(0))
                    STT(qk[:, s2, :], ex[:, s2, :], 1.0, rl[:, s2, :], ALU.min, ALU.add).then_inc(S["feat"], 1)
                if on(b, c, 1) and c > 0:
                    dv.wait_ge(S["s_ps"], carries(b, c, 0))
                    TT(sblk[:], ps[3][:, 0:D], blockmask, ALU.mult).then_inc(S["sblk_ready"], 1)
                if on(b, c, 1) and (c - 1) % TPB:
                    dv.wait_ge(S["intra_ready"], n(1))
                    dv.wait_ge(S["inter_ps"], carries(b, c, 1))
                    TT(osum[:], ps[7][:, 2 * P:2 * P + D], intra[:], ALU.add).then_inc(S["comb_ready"], 1)
                if on(b, c, 0):
                    dv.wait_ge(S["feat"], n(0))
                    if isinstance(b, int) and b == 0 and c == 0:
                        dv.wait_ge(S["ld_const"], 16)
                    v.tensor_tensor_scan(kcum[:], segment, qk[:, c % 2, D:2 * D], 0.0,
                                         ALU.mult, ALU.add).then_inc(S["kc_ready"], 1)
                if on(b, c, 1):
                    o3 = on_t[:].rearrange("p (h e) -> p h e", e=DH)
                    zb = Z[:].unsqueeze(2).broadcast_to([P, H1, DH])
                    dv.wait_ge(S["z_ready"], n(1))
                    if (c - 1) % TPB:
                        dv.wait_ge(S["comb_ready"], carries(b, c, 1))
                        TT(o3, osum[:].rearrange("p (h e) -> p h e", e=DH), zb, ALU.mult).then_inc(S["out_ready"], 1)
                    else:
                        dv.wait_ge(S["intra_ready"], n(1))
                        TT(o3, intra[:].rearrange("p (h e) -> p h e", e=DH), zb, ALU.mult).then_inc(S["out_ready"], 1)
                if on(b, c, 0):
                    dv.wait_ge(S["kc_ready"], n(0))
                    TT(kcq[:, 0:D], kcum[:], qk[:, c % 2, 0:D], ALU.mult).then_inc(S["kq_ready"], 1)
                if on(b, c, 2):
                    s3 = ps[5][:].rearrange("p (h m) -> p h m", m=M)
                    dv.wait_ge(S["sc_ps"], n(2))
                    v.tensor_reduce(mx[:], s3, AX.X, ALU.max).then_inc(S["max_ready"], 1)
                if on(b, c, 0):
                    dv.wait_ge(S["kq_ready"], n(0))
                    v.tensor_reduce(den[:], kcq[:].rearrange("p (d h) -> p h d", d=DH + 1), AX.X,
                                    ALU.add).then_inc(S["den_ready"], 1)
                if on(b, c, 2):
                    s2 = (c - 2) % 2
                    dv.wait_ge(S["max_ready"], n(2))
                    TT(pr[:, s2, :].rearrange("p (h m) -> p h m", m=M), s3,
                       mx[:].unsqueeze(2).broadcast_to([P, H2, M]), ALU.subtract).then_inc(S["sd_ready"], 1)
                if on(b, c, 1):
                    if isinstance(b, int) and b == 0:
                        dv.wait_ge(S["xb_ready"], min(c, 2))
                    dv.wait_ge(S["wo_ps"], n(1))
                    TT(y1[:, (c - 1) % 2, :].unsqueeze(1), ps[7][:, P:P + D].unsqueeze(1), tile(xb_all, 1),
                       ALU.add).then_inc(S["y1_ready"], 1)
                if on(b, c, 3):
                    dv.wait_ge(S["pv_ps"], n(3))
                    TT(y2[:, (c - 3) % 2, :], ps[6][:, 0:D], x1[:, (c - 3) % TPB, :], ALU.add).then_inc(S["y2_ready"], 1)
                if on(b, c, 1):
                    dv.wait_ge(S["y1_ready"], n(1))
                    v.bn_stats(st[:, 0, :], y1[:, (c - 1) % 2, :]).then_inc(S["st1_ready"], 1)
                if on(b, c, 0):
                    dv.wait_ge(S["den_ready"], n(0))
                    v.reciprocal(Z[:], den[:]).then_inc(S["z_ready"], 1)
                if on(b, c, 1):
                    dv.wait_ge(S["st1_ready"], n(1))
                if on(b, c, 3):
                    dv.wait_ge(S["y2_ready"], n(3))
                    v.bn_stats(st[:, 1, :], y2[:, (c - 3) % 2, :]).then_inc(S["st2_ready"], 1)
                if on(b, c, 1):
                    v.bn_aggr(mv1[:, (c - 1) % 2, :], st[:, 0, :]).then_inc(S["var1_ready"], 1)
                if on(b, c, 3):
                    dv.wait_ge(S["st2_ready"], n(3))
                if on(b, c, 2):
                    s2 = (c - 2) % 2
                    dv.wait_ge(S["exp_ready"], n(2))
                    v.tensor_reduce(sm[:], pr[:, s2, :].rearrange("p (h m) -> p h m", m=M), AX.X, ALU.add).then_inc(S["sum_ready"], 1)
                if on(b, c, 3):
                    v.bn_aggr(mv2[:, (c - 3) % 2, :], st[:, 1, :]).then_inc(S["var2_ready"], 1)
                if on(b, c, 4):
                    dv.wait_ge(S["rt_ps"], n(4))
                    v.tensor_copy(tile(logits, 4), ps[4][:, P:P + E].unsqueeze(1)).then_inc(S["logits_ready"], 1)
                if on(b, c, 2):
                    dv.wait_ge(S["sum_ready"], n(2))
                    v.reciprocal(rsm[:, (c - 2) % 2, :], sm[:]).then_inc(S["rsm_ready"], 1)
                if isinstance(b, int) and b == 0 and c == 0:
                    context_copies()
                def q_times_sum(k):
                    dv.wait_ge(S[f"u{k}_ps"], n(0))
                    return TT(qu[:, 512 * k:512 * k + 512].rearrange("p (a e) -> p a e", e=DH),
                              ps[1 + k][:].rearrange("p (a e) -> p a e", e=DH),
                              qk[:, c % 2, 64 * k:64 * k + 64].unsqueeze(2).broadcast_to([P, 64, DH]), ALU.mult)
                if on(b, c, 0):
                    q_times_sum(0)
                if on(b, c, 0):
                    q_times_sum(1).then_inc(S["qu_ready"], 1)

                if isinstance(b, int) and b == B and c == 1:
                    dv.wait_ge(S["ld_tables"], 16)
                    dv.wait_ge(S["logits_ready"], NT - 2)
                    top_two(slice(0, NT - 2))

            tile_steps(dv, step, 4)

            dv.wait_ge(S["logits_ready"], NT)
            top_two(slice(NT - 2, NT))
            TT(hotb[:], onehot[:, 0], onehot[:, 1], ALU.add).then_inc(S["onehot_ready"], 1)
            TT(dl[:], top[:, 1, :], top[:, 0, :], ALU.subtract).then_inc(S["dl_ready"], 1)
            dv.wait_ge(S["rank_ps"], 1)
            totals = ps[0][:, P:2 * P].rearrange("p (n e) -> p e n", e=E)
            v.tensor_reduce(cnt[:], totals, AX.X, ALU.add)
            then(v.tensor_copy(tot[:], totals))
            then(TS(cnti[:], cnt[:], float(P - 1), None, ALU.add))
            then(TS(cnti[:], cnti[:], ~(P - 1), None, ALU.bitwise_and))
            then(TT(pad[:], cnti[:], cnt[:], ALU.subtract))
            then(TT(tot[:, :, NT - 1], tot[:, :, NT - 1], pad[:], ALU.add))
            ones_row = c32[:, C_ONES:C_ONES + P]
            flat = lambda t: t[:].rearrange("p e n -> p (e n)")
            then(v.tensor_tensor_scan(flat(scan), ones_row, flat(tot), 0.0, ALU.mult, ALU.add))
            then(TT(base[:], scan[:], tot[:], ALU.subtract))
            then(TT(pos[:], ps[0][:, 0:P].rearrange("p (n e) -> p n e", e=E), base[:].rearrange("p e n -> p n e"), ALU.add))
            flat2 = lambda t: t.rearrange("p k n e -> p k (n e)")
            then(TT(flat2(posk[:]), flat2(onehot[:]), pos[:].rearrange("p n e -> p (n e)").unsqueeze(1)
                    .broadcast_to([P, TOPK, NT * E]), ALU.mult))
            with nc.allow_low_precision(reason="one nonzero term, a whole number"):
                then(v.tensor_reduce(sloti[:], posk[:].rearrange("p k n e -> p (k n) e"), AX.X, ALU.add))
            TS(rowi[:, 0, :], sloti[:], P - 1, None, ALU.bitwise_and)
            then(TS(rowi[:, 1, :], sloti[:], P.bit_length() - 1, None, ALU.logical_shift_right))
            v.tensor_copy(rowf[:], rowi[:]).then_inc(S["rowf_ready"], 1)
            dv.wait_ge(S["rowf_ready"], 1)
            iota = c32[:, C_IOTA:C_IOTA + P]
            tile_of = rowf[:, 1, :].unsqueeze(2).broadcast_to([P, NPK, NSLOT])
            TT(tilesel[:], iota[:, 0:NSLOT].unsqueeze(1).broadcast_to([P, NPK, NSLOT]), tile_of, ALU.is_equal
               ).then_inc(S["tile_eq"], 1)
            for lo, hi in ROW_CHUNKS:
                TT(rowsel[:, lo:hi, :], iota.unsqueeze(1).broadcast_to([P, hi - lo, P]),
                   rowf[:, 0, lo:hi].unsqueeze(2).broadcast_to([P, hi - lo, P]), ALU.is_equal).then_inc(S["rowsel_ready"], 1)
            dv.wait_ge(S["slot_ps"], 1)
            table = sv[:, 0, :]
            then(v.tensor_copy(table, ps[1][:, 0:NSLOT]))
            then(STT(sv[:, 2, :], table, -1.0, table, ALU.mult, ALU.max))
            TS(src_row[:], sv[:, 2, :], 1.0, -1.0, ALU.max, ALU.add).then_inc(S["src_ready"], 1)
            TS(sv[:, 1, :], sv[:, 2, :], 1.0, -1.0, ALU.max, ALU.add)
            then(TT(endcmp[:], c32[:, C_J128:C_J128 + NSLOT].unsqueeze(2).broadcast_to([P, NSLOT, E]),
                    scan[:, :, NT - 1].unsqueeze(1).broadcast_to([P, NSLOT, E]), ALU.is_ge))
            TS(sv[:, 2, :], table, 0.0, float(NTOK), ALU.is_lt, ALU.mult)
            then(v.tensor_reduce(texp[:], endcmp[:], AX.X, ALU.add))
            TS(texpi[:], texp[:], float(E - 1), None, ALU.min).then_inc(S["texp_ready"], 1)
            STT(sv[:, 3, :], table, 0.0, c32[:, C_DUMMY:C_DUMMY + NSLOT], ALU.is_equal, ALU.mult)
            then(TT(sv[:, 1, :], sv[:, 1, :], sv[:, 2, :], ALU.add))
            TT(dst_row[:], sv[:, 1, :], sv[:, 3, :], ALU.add).then_inc(S["dst_ready"], 1)
            dv.wait_ge(S["e2_ready"], 1)
            then(TS(wtop[:, 1, :], e2[:], 1.0, None, ALU.add))
            then(v.reciprocal(wtop[:, 0, :], wtop[:, 1, :]))
            then(TT(wtop[:, 1, :], wtop[:, 0, :], e2[:], ALU.mult))

            def estep(i, u):
                has = lambda lag: not isinstance(i, int) or 0 <= UNR * i + u - lag < NSLOT
                n = lambda lag: UNR * i + (u - lag + 1)
                sl = (u - 1) % UNR
                if has(3):
                    dv.wait_ge(S["down_ps"], n(3))
                    wait(dv, y_scattered[u], 16 * (i - 1))
                    v.tensor_copy(yx[:, u, :], ps[3][:, 0:D]).then_inc(S["y_ready"], 1)
                if has(1):
                    dv.wait_ge(S["silu_ready"], n(1))
                    dv.wait_ge(S["up_ps"], n(1))
                    wait(dv, S["down_ps"], UNR * i + (u - 1) - UNR + 1)
                    TT(aT[:, sl, :], sg[:, sl, :], ps[1][:, 0:FP], ALU.mult).then_inc(S["a_ready"], 1)

            def weight_diagonals(k, half):
                t = slice(half * (NT // 2), (half + 1) * (NT // 2))
                shape = [P, NT // 2, P]
                TT(diag[k][:, t, :], ident.unsqueeze(1).broadcast_to(shape),
                   wtop[:, k, t].unsqueeze(2).broadcast_to(shape), ALU.mult).then_inc(S["diag_ready"], 1)

            for i in range(2):
                for u in range(UNR):
                    estep(i, u)
                    if UNR * i + u < 4:
                        weight_diagonals((UNR * i + u) // 2, (UNR * i + u) % 2)
            with dv.Fori(2, NIT) as i:
                for u in range(UNR):
                    estep(i, u)
            for u in range(3):
                estep(NIT, u)

            dv.wait_ge(S["x2_ld"], 16)
            dv.wait_ge(y_ld[0], 32)
            for t in range(4):
                last = STT(z0[:, t, :], yk[:, 0, t, :], wtop[:, 0, t:t + 1], x2_all[:, t, :], ALU.mult, ALU.add)
            last.then_inc(S["z_first"], 1)
            dv.wait_ge(S["z_first"], 1)
            for t in range(4):
                last = STT(z0[:, t, :], yk[:, 1, t, :], wtop[:, 1, t:t + 1], z0[:, t, :], ALU.mult, ALU.add)
            last.then_inc(S["z_sum0"], 1)
            for q in range(4):
                tiles = range(4 * q, 4 * q + 4)
                if q == 0:
                    dv.wait_ge(S["z_sum0"], 1)
                else:
                    dv.wait_ge(S["z_sum"], q)
                for t in tiles:
                    last = v.bn_stats(stz[:, t, :], z_of(t))
                last.then_inc(S["z_st"], 1)
                dv.wait_ge(S["z_st"], q + 1)
                for t in tiles:
                    last = v.bn_aggr(mvz[:, t, :], stz[:, t, :])
                last.then_inc(S["z_var"], 1)
            for q in range(2, 4):
                dv.wait_ge(S["z_rs"], q + 1)
                for t in range(4 * q + (0 if q == 2 else 2), 4 * q + 4):
                    last = TS(zn[:, t, :], z_of(t), mvz[:, t, 0:1], rsz[:, t:t + 1], ALU.subtract, ALU.mult)
                last.then_inc(S["zn_last"], 1)


def layout(inputs):
    import numpy as np
    a = {k: np.asarray(v) for k, v in inputs.items()}
    x = a["x"].reshape(NTOK, D)
    dh = lambda w: w.reshape(D, H1, DH).transpose(0, 2, 1).reshape(D, D)
    wqkv = np.concatenate([dh(a["L0_attn_Wq"]), dh(a["L0_attn_Wk"]), a["L0_attn_Wv"]], axis=1)
    pairs = lambda w: w.reshape(-1, 2, NPAIR, DX).transpose(0, 2, 1, 3).reshape(-1, H2 * DX)
    two = lambda v: pairs(v).reshape(NPAIR, P).T
    bq = np.zeros((2, DX, NPAIR, 2), a["L0_xattn_bq"].dtype)
    for t in range(2):
        bq[t, :, :, t] = two(a["L0_xattn_bq"]).reshape(2, DX, NPAIR)[t]
    biases = np.concatenate([two(a["L0_xattn_bk"]), two(a["L0_xattn_bv"]), bq.reshape(P, H2),
                             a["L0_xattn_bo"].reshape(D, 1)], axis=1)
    dn = a["L0_ffn_down_proj"]
    wdn = np.zeros((E, FP, D), dn.dtype)
    wdn[:, :F] = dn
    wdn = wdn.reshape(E, NF, P, D).transpose(2, 0, 1, 3)
    wgu = np.zeros((D, E, 2, FP), dn.dtype)
    wgu[:, :, 0, :F] = a["L0_ffn_gate_proj"].transpose(1, 0, 2)
    wgu[:, :, 1, :F] = a["L0_ffn_up_proj"].transpose(1, 0, 2)
    i, j = np.arange(P)[:, None], np.arange(P)[None, :]
    c = np.zeros((P, NCONST), np.float32)
    c[:, C_ID:C_ID + P] = i == j
    c[:, C_TRI:C_TRI + P] = i <= j
    c[:, C_BLK:C_BLK + P] = (i % H1) == (j // DH)
    c[:, C_SEG:C_SEG + P] = (j % H1) != 0
    c[:, C_REV:C_REV + P] = E - j % E
    c[:, C_IOTA:C_IOTA + P] = j
    c[:, C_ONES:C_ONES + P] = 1
    c[:, C_J128:C_J128 + NSLOT] = P * np.arange(NSLOT)
    kn = np.arange(NPK)[None, :]
    c[:, C_TOK:C_TOK + NPK] = (P * (kn % NT) + i + 1) * np.where(kn < NT, 1, -1)
    c[:, C_DUMMY:C_DUMMY + NSLOT] = TOPK * NTOK + P * np.arange(NSLOT) + i
    c[:, C_HALF:C_HALF + 16] = -0.5
    c[:, C_EPS] = EPS_LN
    c[:, C_NEG] = -1
    cb = np.zeros((P, NCONSTB), np.float32)
    cb[:, B_ID:B_ID + P] = i == j
    cb[:, B_STRICT:B_STRICT + P] = i < j
    cb[:, B_ONE:B_ONE + P] = 1
    cb[:, B_MASK:B_MASK + HM] = np.where(np.arange(HM)[None, :] % M > i, -BIG, 0)
    return {
        "xn": x, "xT": x.T, "wqkv": wqkv, "wo1": a["L0_attn_Wo"], "bo1": a["L0_attn_bo"].reshape(D),
        "consts": c, "constb": cb.astype(mybir.dt.np(BF16)), "ctxT": a["ctx_1024"].reshape(BM, D).T,
        "wk": pairs(a["L0_xattn_Wk"]), "wv": pairs(a["L0_xattn_Wv"]),
        "wqT": pairs(a["L0_xattn_Wq"]).T.reshape(NPAIR, P, D).transpose(1, 0, 2), "biases": biases,
        "wo2": pairs(a["L0_xattn_Wo"].T).T.reshape(NPAIR, P, D).transpose(1, 0, 2), "router": a["L0_ffn_router_w"],
        "wgu": wgu.reshape(D, E * 2 * FP), "wdn": wdn.reshape(P, E * NF * D),
    }


def kernel(**inputs):
    import numpy as np
    import concourse.bacc as bacc
    from concourse.bass_utils import run_bass_kernel_spmd

    nc = bacc.Bacc("TRN2", target_bir_lowering=False, num_devices=1)
    arrays, args = {}, []
    for name, value in layout(inputs).items():
        value = np.ascontiguousarray(value)
        arrays[f"in_{name}"] = value
        args.append(nc.dram_tensor(f"in_{name}", value.shape, mybir.dt.from_np(value.dtype), kind="ExternalInput").ap())
    out = nc.dram_tensor("out_rows", (NTOK, D), F32, kind="ExternalOutput").ap()
    decoder_layer(nc, *args, out)
    r = run_bass_kernel_spmd(nc, [arrays], core_ids=[0])
    return r.results[0]["out_rows"].reshape(B, T, D)
```
